# Optimizing a Trainium2 kernel written in Bass

```python
import numpy as np
import jax
import jax.numpy as jnp

def _softmax(x, axis=-1):
    return jax.nn.softmax(x, axis=axis)

def _gelu(x):
    return jax.nn.gelu(x, approximate=True)

def _silu(x):
    return jax.nn.silu(x)

def _sigmoid(x):
    return jax.nn.sigmoid(x)

def _layernorm(x, axis=-1, eps=1e-05):
    m = jnp.mean(x, axis=axis, keepdims=True)
    v = jnp.var(x, axis=axis, keepdims=True)
    return (x - m) / jnp.sqrt(v + eps)

def _scatter_add(tgt, idx, src, axis=0):
    return tgt.at[idx].add(src)

def _segment_sum(src, seg, n):
    return jax.ops.segment_sum(src, seg, n)
kernel_name = 'mk_gnn_resnorm_d2_gnn_r8_b03b77'

def setup_inputs(seed: int=0):
    np.random.seed(seed)
    _w = jnp.asarray

    def _rec_inputs():
        import jax
        import jax.numpy as jnp
        _gk = jax.random.key(seed)
        x = 8.953e-05 + 1 * jax.random.normal(jax.random.fold_in(_gk, 1), (12500, 16), jnp.float32)
        src = jax.random.randint(jax.random.fold_in(_gk, 2), (400000,), 0, 12500, jnp.int32)
        dst = jnp.minimum((12500 * jax.random.uniform(jax.random.fold_in(_gk, 3), (400000,)) ** 2.0).astype(jnp.int32), 99999)
        _o = jnp.argsort(dst, stable=True)
        src = src[_o]
        dst = dst[_o]
        edge_attr_16 = -0.00010739 + 0.99994 * jax.random.normal(jax.random.fold_in(_gk, 12), (400000, 16), jnp.float32)
        edge_attr_3 = -1.09012e-05 + 0.99985 * jax.random.normal(jax.random.fold_in(_gk, 13), (400000, 3), jnp.float32)
        edge_attr_48 = -3.69585e-06 + 0.999911 * jax.random.normal(jax.random.fold_in(_gk, 14), (400000, 48), jnp.float32)
        edge_type_90 = jax.random.randint(jax.random.fold_in(_gk, 16), (400000,), 0, 90, jnp.int32)
        return (x, src, dst, edge_attr_16, edge_attr_3, edge_attr_48, edge_type_90)
    x, src, dst, edge_attr_16, edge_attr_3, edge_attr_48, edge_type_90 = _rec_inputs()

    def _L0_gnn_setup():
        import jax, jax.numpy as jnp
        import numpy as np
        NS, NV = (16, 4)
        EPS = 1e-05
        N_NODES, N_EDGES = (5000, 50000)

        def _bn_scalar(x, g, b):
            m = x.mean(0)
            v = ((x - m) ** 2).mean(0)
            return (x - m) / jnp.sqrt(v + EPS) * g + b

        def _seg_mean(x, idx, n):
            s = jax.ops.segment_sum(x, idx, num_segments=n)
            c = jax.ops.segment_sum(jnp.ones((idx.shape[0],), x.dtype), idx, num_segments=n)
            return s / jnp.maximum(c, 1.0)[:, None]

        def _edge_weights(edge_attr, w1, b1, w2, b2):
            h = jax.nn.relu(edge_attr @ w1 + b1)
            return h @ w2 + b2

        def _forward(node_attr, edge_attr, edge_vec, fc0_w1, fc0_b1, fc0_w2, fc0_b2, fc1_w1, fc1_b1, fc1_w2, fc1_b2, bn0_gs, bn0_bs, bn0_gv, bn1_gs, bn1_bs, edge_index):
            N = node_attr.shape[0]
            E = edge_attr.shape[0]
            src, dst = (edge_index[0], edge_index[1])
            rhat = edge_vec / (jnp.linalg.norm(edge_vec, axis=-1, keepdims=True) + 1e-12)
            sh1 = rhat * float(np.sqrt(3.0))
            w = _edge_weights(edge_attr, fc0_w1, fc0_b1, fc0_w2, fc0_b2)
            wa = w[:, :NS * NS].reshape(E, NS, NS)
            wb = w[:, NS * NS:].reshape(E, NS, NV)
            x = node_attr[dst]
            inv = float(1.0 / np.sqrt(NS))
            msg_s = jnp.einsum('ei,eij->ej', x, wa) * inv
            msg_v = jnp.einsum('ei,eij,ec->ejc', x, wb, sh1) * inv
            msg = jnp.concatenate([msg_s, msg_v.reshape(E, NV * 3)], axis=-1)
            out = _seg_mean(msg, src, N)
            s0 = _bn_scalar(out[:, :NS], bn0_gs, bn0_bs)
            v0 = out[:, NS:].reshape(N, NV, 3)
            vn = jnp.sqrt((v0 ** 2).mean(axis=(0, 2)) + EPS)
            v0 = v0 / vn[None, :, None] * bn0_gv[None, :, None]
            w = _edge_weights(edge_attr, fc1_w1, fc1_b1, fc1_w2, fc1_b2)
            wa = w[:, :NS * NS].reshape(E, NS, NS)
            wb = w[:, NS * NS:].reshape(E, NV, NS)
            s = s0[dst]
            v = v0[dst]
            path_a = jnp.einsum('ei,eij->ej', s, wa)
            path_b = jnp.einsum('eic,ec,eij->ej', v, sh1, wb) * float(1.0 / np.sqrt(3.0))
            msg = (path_a + path_b) * float(1.0 / np.sqrt(NS + NV))
            node1 = _seg_mean(msg, src, N)
            return _bn_scalar(node1, bn1_gs, bn1_bs)
        key = jax.random.key(seed)
        ks = jax.random.split(key, 8)
        d = 3 * NS
        wn = NS * NS + NS * NV
        g = lambda k, shape, sc: jax.random.normal(k, shape, jnp.float32) * sc
        return {'node_attr': g(ks[0], (N_NODES, NS), 1.0), 'edge_attr': g(ks[1], (N_EDGES, d), 1.0), 'edge_vec': g(ks[2], (N_EDGES, 3), 1.0), 'fc0_w1': g(ks[3], (d, d), d ** (-0.5)), 'fc0_b1': jnp.zeros((d,), jnp.float32), 'fc0_w2': g(ks[4], (d, wn), d ** (-0.5)), 'fc0_b2': jnp.zeros((wn,), jnp.float32), 'fc1_w1': g(ks[5], (d, d), d ** (-0.5)), 'fc1_b1': jnp.zeros((d,), jnp.float32), 'fc1_w2': g(ks[6], (d, wn), d ** (-0.5)), 'fc1_b2': jnp.zeros((wn,), jnp.float32), 'bn0_gs': jnp.ones((NS,), jnp.float32), 'bn0_bs': jnp.zeros((NS,), jnp.float32), 'bn0_gv': jnp.ones((NV,), jnp.float32), 'bn1_gs': jnp.ones((NS,), jnp.float32), 'bn1_bs': jnp.zeros((NS,), jnp.float32), 'edge_index': jax.random.randint(ks[7], (2, N_EDGES), 0, N_NODES)}
    _L0_gnn_all = _L0_gnn_setup()
    _L0_gnn_in = {k: v for k, v in _L0_gnn_all.items() if k in ('fc0_w1', 'fc0_b1', 'fc0_w2', 'fc0_b2', 'fc1_w1', 'fc1_b1', 'fc1_w2', 'fc1_b2', 'bn0_gs', 'bn0_bs', 'bn0_gv', 'bn1_gs', 'bn1_bs')}
    del _L0_gnn_all

    def _L1_gnn_setup():
        import jax, jax.numpy as jnp
        import numpy as np
        N, E, IN, OUT, R, B = (6250, 100000, 16, 16, 90, 30)
        key = jax.random.key(seed)
        ks = jax.random.split(key, 9)
        h = jax.random.normal(ks[0], (N, IN), dtype=jnp.float32)
        he = jax.random.normal(ks[1], (E, IN), dtype=jnp.float32)
        Ws = jax.random.normal(ks[2], (OUT, IN), dtype=jnp.float32) * 0.1
        Wa = jax.random.normal(ks[3], (1, 3 * OUT), dtype=jnp.float32) * 0.1
        weight = jax.random.normal(ks[4], (B, IN, OUT), dtype=jnp.float32) * 0.1
        w_comp = jax.random.normal(ks[5], (R, B), dtype=jnp.float32) * 0.1
        src = jax.random.randint(ks[6], (E,), 0, N)
        dst = jax.random.randint(ks[7], (E,), 0, N)
        rel_type = jax.random.randint(ks[8], (E,), 0, R)
        return {'h': h, 'he': he, 'Ws': Ws, 'Wa': Wa, 'weight': weight, 'w_comp': w_comp, 'src': src, 'dst': dst, 'rel_type': rel_type}
    _L1_gnn_all = _L1_gnn_setup()
    _L1_gnn_in = {k: v for k, v in _L1_gnn_all.items() if k in ('Ws', 'Wa', 'weight', 'w_comp')}
    del _L1_gnn_all
    return {'x': x, 'src': src, 'dst': dst, 'edge_attr_16': edge_attr_16, 'edge_attr_3': edge_attr_3, 'edge_attr_48': edge_attr_48, 'edge_type_90': edge_type_90, 'L0_gnn_fc0_w1': _L0_gnn_in['fc0_w1'], 'L0_gnn_fc0_b1': _L0_gnn_in['fc0_b1'], 'L0_gnn_fc0_w2': _L0_gnn_in['fc0_w2'], 'L0_gnn_fc0_b2': _L0_gnn_in['fc0_b2'], 'L0_gnn_fc1_w1': _L0_gnn_in['fc1_w1'], 'L0_gnn_fc1_b1': _L0_gnn_in['fc1_b1'], 'L0_gnn_fc1_w2': _L0_gnn_in['fc1_w2'], 'L0_gnn_fc1_b2': _L0_gnn_in['fc1_b2'], 'L0_gnn_bn0_gs': _L0_gnn_in['bn0_gs'], 'L0_gnn_bn0_bs': _L0_gnn_in['bn0_bs'], 'L0_gnn_bn0_gv': _L0_gnn_in['bn0_gv'], 'L0_gnn_bn1_gs': _L0_gnn_in['bn1_gs'], 'L0_gnn_bn1_bs': _L0_gnn_in['bn1_bs'], 'L1_gnn_Ws': _L1_gnn_in['Ws'], 'L1_gnn_Wa': _L1_gnn_in['Wa'], 'L1_gnn_weight': _L1_gnn_in['weight'], 'L1_gnn_w_comp': _L1_gnn_in['w_comp']}

def reference(x, src, dst, edge_attr_16, edge_attr_3, edge_attr_48, edge_type_90, L0_gnn_fc0_w1, L0_gnn_fc0_b1, L0_gnn_fc0_w2, L0_gnn_fc0_b2, L0_gnn_fc1_w1, L0_gnn_fc1_b1, L0_gnn_fc1_w2, L0_gnn_fc1_b2, L0_gnn_bn0_gs, L0_gnn_bn0_bs, L0_gnn_bn0_gv, L0_gnn_bn1_gs, L0_gnn_bn1_bs, L1_gnn_Ws, L1_gnn_Wa, L1_gnn_weight, L1_gnn_w_comp):
    import jax
    import jax.numpy as jnp

    def _L0_gnn_ref(node_attr, edge_attr, edge_vec, fc0_w1, fc0_b1, fc0_w2, fc0_b2, fc1_w1, fc1_b1, fc1_w2, fc1_b2, bn0_gs, bn0_bs, bn0_gv, bn1_gs, bn1_bs, edge_index):
        import jax, jax.numpy as jnp
        import numpy as np
        NS, NV = (16, 4)
        EPS = 1e-05
        N_NODES, N_EDGES = (5000, 50000)

        def _bn_scalar(x, g, b):
            m = x.mean(0)
            v = ((x - m) ** 2).mean(0)
            return (x - m) / jnp.sqrt(v + EPS) * g + b

        def _seg_mean(x, idx, n):
            s = jax.ops.segment_sum(x, idx, num_segments=n)
            c = jax.ops.segment_sum(jnp.ones((idx.shape[0],), x.dtype), idx, num_segments=n)
            return s / jnp.maximum(c, 1.0)[:, None]

        def _edge_weights(edge_attr, w1, b1, w2, b2):
            h = jax.nn.relu(edge_attr @ w1 + b1)
            return h @ w2 + b2

        def _forward(node_attr, edge_attr, edge_vec, fc0_w1, fc0_b1, fc0_w2, fc0_b2, fc1_w1, fc1_b1, fc1_w2, fc1_b2, bn0_gs, bn0_bs, bn0_gv, bn1_gs, bn1_bs, edge_index):
            N = node_attr.shape[0]
            E = edge_attr.shape[0]
            src, dst = (edge_index[0], edge_index[1])
            rhat = edge_vec / (jnp.linalg.norm(edge_vec, axis=-1, keepdims=True) + 1e-12)
            sh1 = rhat * float(np.sqrt(3.0))
            w = _edge_weights(edge_attr, fc0_w1, fc0_b1, fc0_w2, fc0_b2)
            wa = w[:, :NS * NS].reshape(E, NS, NS)
            wb = w[:, NS * NS:].reshape(E, NS, NV)
            x = node_attr[dst]
            inv = float(1.0 / np.sqrt(NS))
            msg_s = jnp.einsum('ei,eij->ej', x, wa) * inv
            msg_v = jnp.einsum('ei,eij,ec->ejc', x, wb, sh1) * inv
            msg = jnp.concatenate([msg_s, msg_v.reshape(E, NV * 3)], axis=-1)
            out = _seg_mean(msg, src, N)
            s0 = _bn_scalar(out[:, :NS], bn0_gs, bn0_bs)
            v0 = out[:, NS:].reshape(N, NV, 3)
            vn = jnp.sqrt((v0 ** 2).mean(axis=(0, 2)) + EPS)
            v0 = v0 / vn[None, :, None] * bn0_gv[None, :, None]
            w = _edge_weights(edge_attr, fc1_w1, fc1_b1, fc1_w2, fc1_b2)
            wa = w[:, :NS * NS].reshape(E, NS, NS)
            wb = w[:, NS * NS:].reshape(E, NV, NS)
            s = s0[dst]
            v = v0[dst]
            path_a = jnp.einsum('ei,eij->ej', s, wa)
            path_b = jnp.einsum('eic,ec,eij->ej', v, sh1, wb) * float(1.0 / np.sqrt(3.0))
            msg = (path_a + path_b) * float(1.0 / np.sqrt(NS + NV))
            node1 = _seg_mean(msg, src, N)
            return _bn_scalar(node1, bn1_gs, bn1_bs)
        return _forward(node_attr, edge_attr, edge_vec, fc0_w1, fc0_b1, fc0_w2, fc0_b2, fc1_w1, fc1_b1, fc1_w2, fc1_b2, bn0_gs, bn0_bs, bn0_gv, bn1_gs, bn1_bs, edge_index)

    def _L1_gnn_ref(h, he, Ws, Wa, weight, w_comp, src, dst, rel_type):
        import jax, jax.numpy as jnp
        import numpy as np
        N, E, IN, OUT, R, B = (6250, 100000, 16, 16, 90, 30)
        n_nodes, in_dim = h.shape
        num_bases, _, out_dim = weight.shape
        num_rels = w_comp.shape[0]
        V = weight.reshape(in_dim, num_bases, out_dim)
        W_rel = jnp.matmul(w_comp, V).reshape(num_rels, in_dim, out_dim)
        h_src = h[src]
        z_src = h_src @ Ws.T
        z_dst = h[dst] @ Ws.T
        z_e = he @ Ws.T
        e = jnp.concatenate([z_src, z_e, z_dst], axis=1) @ Wa.T
        msg = jnp.einsum('ei,eio->eo', h_src, W_rel[rel_type]) * e
        h_out = jax.ops.segment_sum(msg, dst, num_segments=n_nodes)
        return h_out
    edge_index = jnp.stack([src, dst])
    x = _layernorm(x + _L0_gnn_ref(x, edge_attr_48, edge_attr_3, L0_gnn_fc0_w1, L0_gnn_fc0_b1, L0_gnn_fc0_w2, L0_gnn_fc0_b2, L0_gnn_fc1_w1, L0_gnn_fc1_b1, L0_gnn_fc1_w2, L0_gnn_fc1_b2, L0_gnn_bn0_gs, L0_gnn_bn0_bs, L0_gnn_bn0_gv, L0_gnn_bn1_gs, L0_gnn_bn1_bs, edge_index), axis=-1)
    x = _layernorm(x + _L1_gnn_ref(x, edge_attr_16, L1_gnn_Ws, L1_gnn_Wa, L1_gnn_weight, L1_gnn_w_comp, src, dst, edge_type_90), axis=-1)
    return x

_drawn_inputs = setup_inputs


def setup_inputs(seed=0):
    import zlib

    import numpy as np

    out = dict(_drawn_inputs(seed))
    spreads = {'L0_gnn_fc0_b1': (0.0, 0.1),
     'L0_gnn_fc0_b2': (0.0, 0.1),
     'L0_gnn_fc1_b1': (0.0, 0.1),
     'L0_gnn_fc1_b2': (0.0, 0.1),
     'L0_gnn_bn0_gs': (1.0, 0.2),
     'L0_gnn_bn0_bs': (0.0, 0.1),
     'L0_gnn_bn0_gv': (1.0, 0.2),
     'L0_gnn_bn1_gs': (1.0, 0.2),
     'L0_gnn_bn1_bs': (0.0, 0.1)}
    factors = {}
    for name, (base, spread) in spreads.items():
        noise = np.random.default_rng([zlib.crc32(name.encode()), seed]).standard_normal(out[name].shape)
        drawn = base * np.exp(spread * noise) if base else spread * noise
        out[name] = jnp.asarray(drawn.astype(out[name].dtype))
    for name, factor in factors.items():
        out[name] = (out[name] * factor).astype(out[name].dtype)
    return out
```

```python
from contextlib import ExitStack

import concourse.bass as bass
from concourse import mybir

FP32 = mybir.dt.float32
BF16 = mybir.dt.bfloat16
I32 = mybir.dt.int32
ALU = mybir.AluOpType
ACT = mybir.ActivationFunctionType
AX = mybir.AxisListType

P = 128
N = 12500
E = 400000
NT = E // P
G = 5
U = 5
GE = G * P
NG = NT // G
TURNS = NG // U
NS, NV = 16, 4
DE = 3 * NS
J = NS + NV
W = NS * J
R, NB = 90, 30
BLK = (N + P - 1) // P
NPAD = BLK * P
LAST = N - (BLK - 1) * P
ROWS = NPAD + P
F0, F1 = 32, 16
EPS = 1e-5
BATCHES = [(0, 2), (2, 5)]
BANK = 512


def need(eng, sem, value):
    if isinstance(value, int) and value <= 0:
        return
    eng.wait_ge(sem, value)


def pipelined(eng, steps):
    peeled = 1 + any(lag for lag, _ in steps)
    def turn_of(it):
        for u in range(U):
            for lag, step in steps:
                turn, slot = it + (u - lag) // U, (u - lag) % U
                if isinstance(turn, int) and turn < 0:
                    continue
                step(turn, slot)
    for it in range(peeled):
        turn_of(it)
    with eng.Fori(peeled, TURNS) as it:
        turn_of(it)
    for u in range(max(lag for lag, _ in steps)):
        for lag, step in steps:
            if lag > u:
                step(TURNS + (u - lag) // U, (u - lag) % U)


def build(nc, x, eaT, heT, ev, src_row, dst_row, type_row, meta, w1, b1, w2, bn0, bn1, ws, wa, basis, comp, out):
    ctx = ExitStack()
    with ctx:
        def sb(name, shape, dt=FP32, on=ctx):
            return on.enter_context(nc.sbuf_tensor(name, shape, dt))

        def ps(name, shape, on=ctx):
            return on.enter_context(nc.psum_tensor(name, shape, FP32))

        def sem(name, on=ctx):
            return on.enter_context(nc.semaphore(name))

        def dram(name, shape, dt=FP32):
            return nc.dram_tensor(name, shape, dt, kind="Internal").ap()

        acc0 = [dram(f"acc0_{g}", [ROWS, F0]) for g in range(G)]
        acc1 = [dram(f"acc1_{g}", [ROWS, F1]) for g in range(G)]
        acc2 = [dram(f"acc2_{g}", [ROWS, F0]) for g in range(G)]
        sv_tab = dram("sv_tab", [NPAD, F0])
        x1_tab = dram("x1_tab", [NPAD, NS])
        rel_flat = dram("rel_flat", [R * NS * NS])

        ones = sb("ones", [P, P])
        upper = sb("upper", [P, P])
        spare = sb("spare", [P, 1])
        spare_i = sb("spare_i", [P, 1], I32)
        lane = sb("lane", [P, 1])
        lane_i = sb("lane_i", [P, 1], I32)
        diff_i = sb("diff_i", [P, P], I32)
        mask = sb("mask", [P, BLK])
        node_i = sb("node_i", [P, BLK], I32)
        w1_sb = sb("w1_sb", [DE, 2, DE])
        b1_sb = sb("b1_sb", [DE, 2])
        w2_sb = sb("w2_sb", [DE + 1, 2, W])
        bn0_sb = sb("bn0_sb", [P, 2 * NS + NV])
        bn1_sb = sb("bn1_sb", [P, 2 * NS])
        ws_sb = sb("ws_sb", [NS, NS])
        wa_sb = sb("wa_sb", [NS, 3])
        wa_rep = sb("wa_rep", [NS, 3, P])
        u_all = sb("u_all", [P, 3, NS])
        u_edge = sb("u_edge", [NS, 1])
        rel_parts = sb("rel_parts", [R, 3, (NS + 1) * NS], BF16)
        rhat = sb("rhat", [P, NT, 3])
        x_sb = sb("x_sb", [P, BLK, NS])
        x1_sb = sb("x1_sb", [P, BLK, NS])
        inv_count = sb("inv_count", [P, BLK])

        with ExitStack() as st:
            zeros = sb("zeros", [P, 2 * ROWS * F0 // P // 2], on=st)
            basis_sb = sb("basis_sb", [NB, NS * NS], on=st)
            comp_sb = sb("comp_sb", [NB, R], on=st)
            rel_p = sb("rel_p", [R, NS * NS], on=st)
            rel_io = sb("rel_io", [R, NS, NS], on=st)
            rel_oi = sb("rel_oi", [R, NS + 1, NS], on=st)
            rest = sb("rest", [R, 2, (NS + 1) * NS], on=st)
            ev_sb = sb("ev_sb", [P, NT, 3], on=st)
            len2 = sb("len2", [P, NT], on=st)
            root = sb("root", [P, NT], on=st)
            inv = sb("inv", [P, NT], on=st)
            ps_rel = ps("ps_rel", [R, NS * NS], on=st)
            ps_u = ps("ps_u", [P, 3, NS], on=st)
            ps_ue = ps("ps_ue", [NS, 1], on=st)
            loaded = sem("loaded", st)
            ev_in = sem("ev_in", st)
            iotas = sem("iotas", st)
            zeroed = sem("zeroed", st)
            cleared = sem("cleared", st)
            wa_ready = sem("wa_ready", st)
            products = sem("products", st)
            rel_copied = sem("rel_copied", st)
            rel_out = sem("rel_out", st)
            rel_in = sem("rel_in", st)
            squared = sem("squared", st)
            rooted = sem("rooted", st)
            step = sem("step", st)
            block = st.enter_context(nc.Block())
            n_loads = [0]

            @block.sync
            def _(sp):
                def load(dst, src):
                    sp.dma_start(dst, src).then_inc(loaded, 16)
                    n_loads[0] += 1
                sp.dma_start(ev_sb[:], ev).then_inc(ev_in, 16)
                load(w1_sb[:], w1)
                load(b1_sb[:], b1)
                load(w2_sb[:], w2)
                load(bn0_sb[:], bn0.partition_broadcast(P))
                load(bn1_sb[:], bn1.partition_broadcast(P))
                load(ws_sb[:], ws)
                load(wa_sb[:], wa)
                load(basis_sb[:], basis)
                load(comp_sb[:], comp)
                load(x_sb[:, 0:BLK - 1, :], x[0:(BLK - 1) * P, :].rearrange("(b p) f -> p b f", p=P))
                sp.wait_ge(zeroed, 2)
                load(x_sb[0:LAST, BLK - 1, :], x[(BLK - 1) * P:N, :])
                for a in acc0 + acc1 + acc2:
                    width = ROWS * a.shape[1] // P
                    sp.dma_start(a.rearrange("(p r) f -> p (r f)", p=P), zeros[:, 0:width]).then_inc(cleared, 16)
                sp.wait_ge(rel_copied, 1)
                sp.dma_start(rel_flat.rearrange("(i r o) -> r i o", i=NS, r=R),
                             rel_p[:].rearrange("r (i o) -> r i o", i=NS)).then_inc(rel_out, 16)
                sp.wait_ge(rel_out, 16)
                sp.dma_start(rel_io[:], rel_flat.rearrange("(r i o) -> r i o", r=R, i=NS)).then_inc(rel_in, 16)
                sp.wait_ge(loaded, 16 * n_loads[0])
                sp.wait_ge(cleared, 16 * 3 * G)

            @block.gpsimd
            def _(pool):
                nc.gpsimd.iota(diff_i[:], pattern=[[1, P]], base=0, channel_multiplier=-1)
                nc.gpsimd.iota(lane_i[:], pattern=[[0, 1]], base=0, channel_multiplier=1)
                nc.gpsimd.iota(spare_i[:], pattern=[[0, 1]], base=NPAD, channel_multiplier=1)
                nc.gpsimd.iota(node_i[:], pattern=[[P, BLK]], base=0, channel_multiplier=1).then_inc(iotas, 1)

            @block.vector
            def _(dve):
                done = [0]

                def chain(ins):
                    ins.then_inc(step, 1)
                    done[0] += 1
                    dve.wait_ge(step, done[0])
                nc.vector.memset(zeros[:], 0.0).then_inc(zeroed, 1)
                nc.vector.memset(x_sb[:, BLK - 1, :], 0.0).then_inc(zeroed, 1)
                nc.vector.memset(ones[:], 1.0)
                dve.wait_ge(iotas, 1)
                nc.vector.tensor_scalar(upper[:], diff_i[:], 0.0, None, ALU.is_ge)
                nc.vector.tensor_copy(lane[:], lane_i[:])
                nc.vector.tensor_copy(spare[:], spare_i[:])
                nc.vector.tensor_scalar(mask[:], node_i[:], float(N), None, ALU.is_lt)
                dve.wait_ge(loaded, 16 * n_loads[0])
                nc.vector.tensor_copy(wa_rep[:], wa_sb[:, :].unsqueeze(2).broadcast_to([NS, 3, P])).then_inc(wa_ready, 1)
                dve.wait_ge(ev_in, 16)
                chain(nc.vector.tensor_tensor(rhat[:], ev_sb[:], ev_sb[:], ALU.mult))
                nc.vector.reduce_sum(len2[:], rhat[:], AX.X).then_inc(squared, 1)
                dve.wait_ge(products, 1)
                nc.vector.tensor_copy(rel_p[:], ps_rel[:]).then_inc(rel_copied, 1)
                nc.vector.tensor_copy(u_all[:], ps_u[:])
                chain(nc.vector.tensor_copy(u_edge[:], ps_ue[:]))
                dve.wait_ge(rooted, 1)
                chain(nc.vector.tensor_scalar(inv[:], root[:], 1e-30, None, ALU.add))
                chain(nc.vector.reciprocal(inv[:], inv[:]))
                chain(nc.vector.tensor_tensor(inv[:], inv[:], len2[:], ALU.mult))
                chain(nc.vector.tensor_tensor(root[:], root[:], inv[:], ALU.add))
                chain(nc.vector.tensor_scalar(root[:], root[:], 0.5, 1e-12, ALU.mult, ALU.add))
                chain(nc.vector.reciprocal(inv[:], root[:]))
                nc.vector.tensor_tensor(rhat[:], ev_sb[:], inv[:, :].unsqueeze(2).broadcast_to([P, NT, 3]), ALU.mult)
                dve.wait_ge(rel_in, 16)
                nc.vector.tensor_copy(rel_oi[:, 1:, :], rel_io[:].rearrange("r i o -> r o i"))
                chain(nc.vector.tensor_copy(rel_oi[:, 0, :], u_all[0:R, 0, :]))
                flat = rel_oi[:].rearrange("r o i -> r (o i)")
                chain(nc.vector.tensor_copy(rel_parts[:, 0, :], flat))
                chain(nc.vector.tensor_tensor(rest[:, 0, :], flat, rel_parts[:, 0, :], ALU.subtract))
                chain(nc.vector.tensor_copy(rel_parts[:, 1, :], rest[:, 0, :]))
                chain(nc.vector.tensor_tensor(rest[:, 1, :], rest[:, 0, :], rel_parts[:, 1, :], ALU.subtract))
                chain(nc.vector.tensor_copy(rel_parts[:, 2, :], rest[:, 1, :]))

            @block.scalar
            def _(act):
                act.wait_ge(squared, 1)
                nc.scalar.activation(root[:], len2[:], ACT.Sqrt).then_inc(rooted, 1)

            @block.tensor
            def _(pe):
                pe.wait_ge(wa_ready, 1)
                nc.tensor.matmul(ps_rel[:], comp_sb[:], basis_sb[:], start=True, stop=True)
                for k in range(3):
                    nc.tensor.matmul(ps_u[:, k, :], wa_rep[:, k, :], ws_sb[:], start=True, stop=True)
                nc.tensor.matmul(ps_ue[:], ws_sb[:], wa_sb[:, 1:2], start=True, stop=True).then_inc(products, 1)

        def edge_pass(layer):
            conv = layer < 2
            gw = (NS, F0, NS)[layer]
            table = (x, sv_tab, x1_tab)[layer]
            ni, nj = ((NS, J), (J, NS), (NS, NS + 1))[layer]
            wcols = ni * nj
            fw = (F0, F1, F0)[layer]
            acc = (acc0, acc1, acc2)[layer]
            first = (4, 0, 1)[layer]
            mw = first + fw
            key_row = src_row if conv else dst_row
            to, frm = (1, 0) if conv else (0, 1)
            with ExitStack() as st:
                name = lambda s: f"{s}_{layer}"
                feat = sb(name("feat"), [DE if conv else NS, U, GE], on=st)
                keys = sb(name("keys"), [P, U, GE], I32, on=st)
                idx = sb(name("idx"), [P, U, 2, G], I32, on=st)
                rows = sb(name("rows"), [P, U, G, gw], on=st)
                same = sb(name("same"), [P, U, G, P], on=st)
                later = sb(name("later"), [P, U, G], on=st)
                last = sb(name("last"), [P, U, G], on=st)
                dest = sb(name("dest"), [P, U, G], I32, on=st)
                prod = sb(name("prod"), [P, U, G, wcols], on=st)
                msg = sb(name("msg"), [P, U, G, mw], on=st)
                sums = sb(name("sums"), [P, U, G, fw], on=st)
                ps_w = ps(name("ps_w"), [P, G, BANK], on=st)
                ps_sum = ps(name("ps_sum"), [P, BANK], on=st)
                if conv:
                    hid = sb(name("hid"), [64, U, GE], on=st)
                    ps_h = ps(name("ps_h"), [DE, 2, BANK], on=st)
                else:
                    types = sb(name("types"), [R, U, GE], I32, on=st)
                    onehot = sb(name("onehot"), [R, U, GE], BF16, on=st)
                    ps_e = ps(name("ps_e"), [P, BANK], on=st)
                    att = sb(name("att"), [P, U, G], on=st)
                    edge = sb(name("edge"), [P, U, G], on=st)
                if layer == 1:
                    vr = sb(name("vr"), [P, U, G, 3 * NV], on=st)
                in_ready = [sem(name(f"in_ready{u}"), st) for u in range(U)]
                rows_ready = [sem(name(f"rows_ready{u}"), st) for u in range(U)]
                added = [sem(name(f"added{g}"), st) for g in range(G)]
                preset = sem(name("preset"), st)
                passed = sem(name("passed"), st)
                hid_mm = sem(name("hid_mm"), st)
                hid_ready = sem(name("hid_ready"), st)
                edge_ready = sem(name("edge_ready"), st)
                w_done = sem(name("w_done"), st)
                mult_done = sem(name("mult_done"), st)
                same_ready = sem(name("same_ready"), st)
                msg_ready = sem(name("msg_ready"), st)
                summed = sem(name("summed"), st)
                sums_ready = sem(name("sums_ready"), st)
                last_ready = sem(name("last_ready"), st)
                offset_ready = sem(name("offset_ready"), st)
                turned = sem(name("turned"), st)
                reduced = sem(name("reduced"), st)
                att_ready = sem(name("att_ready"), st)
                block = st.enter_context(nc.Block())

                @block.sync
                def _(sp):
                    def load(turn, u):
                        n = turn * U + u
                        need(sp, hid_mm, n - U + 1)
                        if not conv:
                            need(sp, hid_ready, n - U + 1)
                        need(sp, offset_ready, n - U + 1)
                        sp.sem_inc(passed)
                        need(sp, mult_done, 2 * (n - U + 1))
                        sp.sem_inc(passed)
                        e0 = n * GE
                        sp.dma_start(feat[:, u, :], (eaT if conv else heT)[:, bass.ds(e0, GE)]).then_inc(in_ready[u], 16)
                        sp.dma_start(keys[:, u, :], key_row[:, bass.ds(e0, GE)].partition_broadcast(P)).then_inc(in_ready[u], 16)
                        sp.dma_start(idx[:, u], meta[bass.ds(n, 1)].rearrange("a p k g -> (a p) k g")).then_inc(in_ready[u], 16)
                        if not conv:
                            sp.dma_start(types[:, u, :], type_row[:, bass.ds(e0, GE)].partition_broadcast(R)).then_inc(in_ready[u], 16)
                    pipelined(sp, [(0, load)])

                loads = 3 if conv else 4

                @block.gpsimd
                def _(pool):
                    def gather(turn, u):
                        n = turn * U + u
                        need(pool, in_ready[u], 16 * loads * (turn + 1))
                        need(pool, mult_done, 2 * (n - U + 1))
                        pool.sem_inc(passed)
                        for g in range(G):
                            nc.gpsimd.indirect_dma_start(
                                out=rows[:, u, g, :], out_offset=None, in_=table,
                                in_offset=bass.IndirectOffsetOnAxis(ap=idx[:, u, frm, g:g + 1], axis=0),
                            ).then_inc(rows_ready[u], 16)

                    def add(turn, u):
                        n = turn * U + u
                        need(pool, sums_ready, 2 * (n + 1))
                        for g in range(G):
                            need(pool, added[g], 16 * n)
                            pool.sem_inc(passed)
                            nc.gpsimd.indirect_dma_start(
                                out=acc[g], out_offset=bass.IndirectOffsetOnAxis(ap=dest[:, u, g:g + 1], axis=0),
                                in_=sums[:, u, g, :], in_offset=None, compute_op=ALU.add,
                            ).then_inc(added[g], 16)
                    pipelined(pool, [(0, gather), (4, add)])
                    for g in range(G):
                        pool.wait_ge(added[g], 16 * NG)

                @block.tensor
                def _(pe):
                    def hidden(turn, u):
                        n = turn * U + u
                        need(pe, in_ready[u], 16 * loads * (turn + 1))
                        if conv:
                            need(pe, hid_ready, n)
                            pe.sem_inc(passed)
                            for c in range(2):
                                mm = nc.tensor.matmul(ps_h[:, c, 0:GE // 2], w1_sb[:, layer, :],
                                                      feat[:, u, c * (GE // 2):(c + 1) * (GE // 2)], start=True, stop=True)
                        else:
                            need(pe, edge_ready, n)
                            pe.sem_inc(passed)
                            for g in range(G):
                                mm = nc.tensor.matmul(ps_e[:, g:g + 1], feat[:, u, g * P:(g + 1) * P], u_edge[:],
                                                      start=True, stop=True)
                        mm.then_inc(hid_mm, 1)

                    def weights(turn, u):
                        n = turn * U + u
                        need(pe, hid_ready, n + 1)
                        if conv:
                            need(pe, preset, 1)
                        for b, (g0, g1) in enumerate(BATCHES):
                            need(pe, mult_done, 2 * n - 1 + b)
                            for g in range(g0, g1):
                                if conv:
                                    mm = nc.tensor.matmul(ps_w[:, g, 0:wcols], hid[0:DE + 1, u, g * P:(g + 1) * P],
                                                          w2_sb[:, layer, :], start=True, stop=True)
                                else:
                                    for k in range(3):
                                        mm = nc.tensor.matmul(ps_w[:, g, 0:wcols], onehot[:, u, g * P:(g + 1) * P],
                                                              rel_parts[:, k, :], start=k == 0, stop=k == 2)
                            mm.then_inc(w_done, 1)

                    def sum_same(turn, u):
                        n = turn * U + u
                        need(pe, msg_ready, n + 1)
                        need(pe, same_ready, n + 1)
                        need(pe, preset, 1)
                        need(pe, sums_ready, 2 * n)
                        for g in range(G):
                            mm = nc.tensor.matmul(ps_sum[:, g * fw:(g + 1) * fw], same[:, u, g, :],
                                                  msg[:, u, g, first:first + fw], start=True, stop=True)
                        mm.then_inc(summed, 1)
                    pipelined(pe, [(0, hidden), (1, weights), (3, sum_same)])

                @block.scalar
                def _(act):
                    def relu(turn, u):
                        n = turn * U + u
                        need(act, hid_mm, n + 1)
                        need(act, preset, 1)
                        need(act, w_done, 2 * (n - U + 1))
                        nc.scalar.activation(hid[0:DE, u, :].rearrange("p (c e) -> p c e", c=2), ps_h[:, :, 0:GE // 2],
                                             ACT.Relu, bias=b1_sb[:, layer:layer + 1]).then_inc(hid_ready, 1)

                    def take_edges(turn, u):
                        n = turn * U + u
                        need(act, hid_mm, n + 1)
                        need(act, msg_ready, n - U + 1)
                        nc.scalar.activation(edge[:, u, :], ps_e[:, 0:G], ACT.Copy).then_inc(edge_ready, 1)

                    def take_sums(turn, u):
                        n = turn * U + u
                        need(act, summed, n + 1)
                        for g in range(G):
                            need(act, added[g], 16 * (n - U + 1))
                        nc.scalar.activation(sums[:, u].rearrange("p g f -> p (g f)"), ps_sum[:, 0:G * fw],
                                             ACT.Copy).then_inc(sums_ready, 1)
                        need(act, offset_ready, n + 1)
                        nc.scalar.activation(dest[:, u, :], later[:, u, :], ACT.Identity, bias=spare[:]).then_inc(sums_ready, 1)
                    pipelined(act, [(0, relu if conv else take_edges), (3, take_sums)])

                @block.vector
                def _(dve):
                    if conv:
                        nc.vector.memset(hid[32:64, :, :], 1.0)
                    if layer == 0:
                        nc.vector.memset(msg[:, :, :, J + 3 * NV:J + 3 * NV + 1], 1.0)
                        nc.vector.memset(msg[:, :, :, J + 3 * NV + 1:], 0.0)
                    nc.vector.drain().then_inc(preset, 1)

                    def find_same(turn, u):
                        n = turn * U + u
                        need(dve, in_ready[u], 16 * loads * (turn + 1))
                        need(dve, summed, n - U + 1)
                        need(dve, sums_ready, 2 * (n - U + 1))
                        if not conv:
                            need(dve, w_done, 2 * (n - U + 1))
                            nc.vector.tensor_scalar(onehot[:, u, :], types[:, u, :], lane[0:R, :], None,
                                                    ALU.is_equal).then_inc(hid_ready, 1)
                        for g in range(G):
                            ins = nc.vector.scalar_tensor_tensor(
                                out=same[:, u, g, :], in0=keys[:, u, g * P:(g + 1) * P], scalar=idx[:, u, to, g:g + 1],
                                in1=upper[:], op0=ALU.is_equal, op1=ALU.mult, accum_out=later[:, u, g:g + 1])
                        ins.then_inc(same_ready, 1)

                    def find_dest(turn, u):
                        n = turn * U + u
                        need(dve, same_ready, n + 1)
                        nc.vector.tensor_scalar(last[:, u, :], later[:, u, :], 1.0, None, ALU.is_equal).then_inc(last_ready, 1)
                        need(dve, last_ready, n + 1)
                        nc.vector.scalar_tensor_tensor(out=later[:, u, :], in0=idx[:, u, to, :], scalar=spare[:], in1=last[:, u, :],
                                                       op0=ALU.subtract, op1=ALU.mult).then_inc(offset_ready, 1)

                    def multiply(turn, u):
                        n = turn * U + u
                        need(dve, rows_ready[u], 16 * G * (turn + 1))
                        if layer == 1:
                            dirs = rhat[:, bass.ds(n * G, G), :].unsqueeze(2).broadcast_to([P, G, NV, 3])
                            nc.vector.tensor_tensor(vr[:, u].rearrange("p g (k c) -> p g k c", c=3),
                                                    rows[:, u, :, J:F0].rearrange("p g (k c) -> p g k c", c=3),
                                                    dirs, ALU.mult).then_inc(turned, 1)
                            need(dve, turned, 2 * n + 1)
                            nc.vector.reduce_sum(rows[:, u, :, NS:J], vr[:, u].rearrange("p g (k c) -> p g k c", c=3),
                                                 AX.X).then_inc(turned, 1)
                            need(dve, turned, 2 * n + 2)
                        for b, (g0, g1) in enumerate(BATCHES):
                            need(dve, w_done, 2 * n + 1 + b)
                            nc.vector.tensor_tensor(
                                prod[:, u, g0:g1, :].rearrange("p g (j i) -> p g j i", i=ni),
                                ps_w[:, g0:g1, 0:wcols].rearrange("p g (j i) -> p g j i", i=ni),
                                rows[:, u, g0:g1, 0:ni].unsqueeze(2).broadcast_to([P, g1 - g0, nj, ni]),
                                ALU.mult).then_inc(mult_done, 1)

                    def message(turn, u):
                        n = turn * U + u
                        need(dve, mult_done, 2 * (n + 1))
                        need(dve, summed, n - U + 1)
                        if layer == 0:
                            nc.vector.reduce_sum(msg[:, u, :, 0:J], prod[:, u].rearrange("p g (j i) -> p g j i", i=ni),
                                                 AX.X).then_inc(reduced, 1)
                            need(dve, reduced, n + 1)
                            vk = msg[:, u, :, 0:NV].unsqueeze(3).broadcast_to([P, G, NV, 3])
                            dirs = rhat[:, bass.ds(n * G, G), :].unsqueeze(2).broadcast_to([P, G, NV, 3])
                            nc.vector.tensor_tensor(msg[:, u, :, J:J + 3 * NV].rearrange("p g (k c) -> p g k c", c=3),
                                                    vk, dirs, ALU.mult).then_inc(msg_ready, 1)
                        elif layer == 1:
                            nc.vector.reduce_sum(msg[:, u], prod[:, u].rearrange("p g (j i) -> p g j i", i=ni),
                                                 AX.X).then_inc(msg_ready, 1)
                        else:
                            nc.vector.reduce_sum(msg[:, u, :, 0:nj], prod[:, u].rearrange("p g (j i) -> p g j i", i=ni),
                                                 AX.X).then_inc(reduced, 1)
                            need(dve, reduced, n + 1)
                            need(dve, edge_ready, n + 1)
                            nc.vector.tensor_tensor(att[:, u, :], msg[:, u, :, 0], edge[:, u, :],
                                                    ALU.add).then_inc(att_ready, 1)
                            need(dve, att_ready, n + 1)
                            nc.vector.tensor_tensor(msg[:, u, :, nj:], msg[:, u, :, 1:nj],
                                                    att[:, u, :].unsqueeze(2).broadcast_to([P, G, NS]),
                                                    ALU.mult).then_inc(msg_ready, 1)
                    pipelined(dve, [(0, find_same), (0, find_dest), (0, multiply), (1, message)])

        def node_stage(layer):
            fw = (F0, F1, F0)[layer]
            acc = (acc0, acc1, acc2)[layer]
            with ExitStack() as st:
                name = lambda s: f"{s}_n{layer}"
                parts = sb(name("parts"), [P, G, BLK, fw], on=st)
                tot = sb(name("tot"), [P, BLK, fw], on=st)
                y = sb(name("y"), [P, BLK, F0], on=st)
                sq = sb(name("sq"), [P, BLK, F0], on=st)
                row = sb(name("row"), [P, 4, F0], on=st)
                per = sb(name("per"), [P, 6, BLK], on=st)
                ps_t = ps(name("ps_t"), [P, 2, BANK], on=st)
                in_ready = sem(name("in_ready"), st)
                partial = sem(name("partial"), st)
                total = sem(name("total"), st)
                square = sem(name("square"), st)
                rooted = sem(name("rooted"), st)
                step = sem(name("step"), st)
                stored = sem(name("stored"), st)
                finished = sem(name("finished"), st)
                n_tot = (2, 2, 0)[layer]
                roots = (1, 2, 1)[layer]
                block = st.enter_context(nc.Block())
                ncol = J if layer == 0 else NS
                of_columns = (row[:, 1, 0:ncol], row[:, 2, 0:ncol])
                of_nodes = (per[:, 1, :], per[:, 2, :])
                rounds = ([of_columns], [of_columns, of_nodes], [of_nodes])[layer]

                @block.sync
                def _(sp):
                    for g in range(G):
                        sp.dma_start(parts[:, g], acc[g][0:NPAD, :].rearrange("(b p) f -> p b f", p=P)).then_inc(in_ready, 16)
                    sp.wait_ge(finished, 1)
                    if layer == 0:
                        sp.dma_start(sv_tab.rearrange("(b p) f -> p b f", p=P), y[:]).then_inc(stored, 16)
                        sp.wait_ge(stored, 16)
                    elif layer == 1:
                        sp.dma_start(x1_tab.rearrange("(b p) f -> p b f", p=P), x1_sb[:]).then_inc(stored, 16)
                        sp.wait_ge(stored, 16)
                    else:
                        sp.dma_start(out[0:(BLK - 1) * P, :].rearrange("(b p) f -> p b f", p=P),
                                     y[:, 0:BLK - 1, 0:NS]).then_inc(stored, 16)
                        sp.dma_start(out[(BLK - 1) * P:N, :], y[0:LAST, BLK - 1, 0:NS]).then_inc(stored, 16)
                        sp.wait_ge(stored, 32)

                @block.tensor
                def _(pe):
                    for k in range(n_tot):
                        pe.wait_ge(partial, k + 1)
                        nc.tensor.matmul(ps_t[:, k, 0:F0], ones[:], row[:, 0, :], start=True, stop=True).then_inc(total, 1)

                @block.scalar
                def _(act):
                    for k, (square_of, root_of) in enumerate(rounds):
                        act.wait_ge(square, k + 1)
                        nc.scalar.activation(root_of, square_of, ACT.Sqrt).then_inc(rooted, 1)

                @block.vector
                def _(dve):
                    done = [0]

                    def chain(ins):
                        ins.then_inc(step, 1)
                        done[0] += 1
                        dve.wait_ge(step, done[0])

                    def over_nodes(part, k):
                        nc.vector.drain().then_inc(partial, 1)
                        dve.wait_ge(total, k + 1)

                    def inverse_root(a, root, out_, spare_, k):
                        nc.vector.drain().then_inc(square, 1)
                        dve.wait_ge(rooted, k + 1)
                        chain(nc.vector.reciprocal(spare_, root))
                        chain(nc.vector.tensor_tensor(spare_, spare_, a, ALU.mult))
                        chain(nc.vector.tensor_tensor(spare_, spare_, root, ALU.add))
                        chain(nc.vector.tensor_scalar(spare_, spare_, 0.5, None, ALU.mult))
                        chain(nc.vector.reciprocal(out_, spare_))

                    def rows_of(a, n=None):
                        return a.unsqueeze(1).broadcast_to([P, BLK, a.shape[-1]])

                    def layernorm(dst, src):
                        chain(nc.vector.reduce_sum(per[:, 0, :], src, AX.X))
                        chain(nc.vector.tensor_scalar(per[:, 0, :], per[:, 0, :], 1.0 / NS, None, ALU.mult))
                        chain(nc.vector.tensor_tensor(src, src, per[:, 0, :].unsqueeze(2).broadcast_to([P, BLK, NS]), ALU.subtract))
                        chain(nc.vector.tensor_tensor(sq[:, :, 0:NS], src, src, ALU.mult))
                        chain(nc.vector.reduce_sum(per[:, 1, :], sq[:, :, 0:NS], AX.X))
                        chain(nc.vector.tensor_scalar(per[:, 1, :], per[:, 1, :], 1.0 / NS, EPS, ALU.mult, ALU.add))
                        inverse_root(per[:, 1, :], per[:, 2, :], per[:, 3, :], per[:, 4, :], roots - 1)
                        chain(nc.vector.tensor_tensor(dst, src, per[:, 3, :].unsqueeze(2).broadcast_to([P, BLK, NS]), ALU.mult))

                    dve.wait_ge(in_ready, 16 * G)
                    chain(nc.vector.tensor_tensor(tot[:], parts[:, 0], parts[:, 1], ALU.add))
                    for g in range(2, G):
                        chain(nc.vector.tensor_tensor(tot[:], tot[:], parts[:, g], ALU.add))
                    if layer < 2:
                        if layer == 0:
                            chain(nc.vector.tensor_scalar(inv_count[:], tot[:, :, NS + 3 * NV], 1.0, None, ALU.max))
                            chain(nc.vector.reciprocal(inv_count[:], inv_count[:]))
                        scale = 0.25 if layer == 0 else float((NS + NV) ** -0.5)
                        chain(nc.vector.tensor_scalar(per[:, 5, :], inv_count[:], scale, None, ALU.mult))
                        chain(nc.vector.tensor_tensor(y[:, :, 0:NS], tot[:, :, 0:NS],
                                                      per[:, 5, :].unsqueeze(2).broadcast_to([P, BLK, NS]), ALU.mult))
                        chain(nc.vector.memset(row[:], 0.0))
                        chain(nc.vector.reduce_sum(row[:, 0, 0:NS], y[:, :, 0:NS].rearrange("p b f -> p f b"), AX.X))
                        over_nodes(None, 0)
                        chain(nc.vector.tensor_scalar(row[:, 3, 0:NS], ps_t[:, 0, 0:NS], 1.0 / N, None, ALU.mult))
                        chain(nc.vector.tensor_tensor(y[:, :, 0:NS], y[:, :, 0:NS], rows_of(row[:, 3, 0:NS]), ALU.subtract))
                        chain(nc.vector.tensor_tensor(y[:, :, 0:NS], y[:, :, 0:NS],
                                                      mask[:, :].unsqueeze(2).broadcast_to([P, BLK, NS]), ALU.mult))
                        chain(nc.vector.tensor_tensor(sq[:, :, 0:NS], y[:, :, 0:NS], y[:, :, 0:NS], ALU.mult))
                        chain(nc.vector.reduce_sum(row[:, 0, 0:NS], sq[:, :, 0:NS].rearrange("p b f -> p f b"), AX.X))
                        if layer == 0:
                            chain(nc.vector.tensor_scalar(per[:, 5, :], inv_count[:], 0.25 * 3.0 ** 0.5, None, ALU.mult))
                            chain(nc.vector.tensor_tensor(y[:, :, J:F0], tot[:, :, NS:NS + 3 * NV],
                                                          per[:, 5, :].unsqueeze(2).broadcast_to([P, BLK, 3 * NV]), ALU.mult))
                            chain(nc.vector.tensor_tensor(sq[:, :, J:F0], y[:, :, J:F0], y[:, :, J:F0], ALU.mult))
                            chain(nc.vector.reduce_sum(row[:, 1, 0:3 * NV], sq[:, :, J:F0].rearrange("p b f -> p f b"), AX.X))
                            chain(nc.vector.reduce_sum(row[:, 0, NS:J], row[:, 1, 0:3 * NV].rearrange("p (k c) -> p k c", c=3), AX.X))
                        over_nodes(None, 1)
                        chain(nc.vector.tensor_scalar(row[:, 1, 0:NS], ps_t[:, 1, 0:NS], 1.0 / N, EPS, ALU.mult, ALU.add))
                        if layer == 0:
                            chain(nc.vector.tensor_scalar(row[:, 1, NS:J], ps_t[:, 1, NS:J], 1.0 / (3 * N), EPS, ALU.mult, ALU.add))
                        inverse_root(row[:, 1, 0:ncol], row[:, 2, 0:ncol], row[:, 3, 0:ncol], row[:, 0, 0:ncol], 0)
                        gains = bn0_sb if layer == 0 else bn1_sb
                        chain(nc.vector.tensor_tensor(row[:, 0, 0:NS], row[:, 3, 0:NS], gains[:, 0:NS], ALU.mult))
                        chain(nc.vector.tensor_tensor(y[:, :, 0:NS], y[:, :, 0:NS], rows_of(row[:, 0, 0:NS]), ALU.mult))
                        chain(nc.vector.tensor_tensor(y[:, :, 0:NS], y[:, :, 0:NS], rows_of(gains[:, NS:2 * NS]), ALU.add))
                        if layer == 0:
                            chain(nc.vector.tensor_tensor(row[:, 0, NS:J], row[:, 3, NS:J], gains[:, 2 * NS:], ALU.mult))
                            chain(nc.vector.tensor_tensor(
                                y[:, :, J:F0].rearrange("p b (k c) -> p b k c", c=3), y[:, :, J:F0].rearrange("p b (k c) -> p b k c", c=3),
                                row[:, 0, NS:J].unsqueeze(1).unsqueeze(3).broadcast_to([P, BLK, NV, 3]), ALU.mult))
                            nc.vector.memset(y[:, :, NS:J], 0.0)
                        else:
                            chain(nc.vector.tensor_tensor(y[:, :, 0:NS], y[:, :, 0:NS], x_sb[:], ALU.add))
                            layernorm(x1_sb[:], y[:, :, 0:NS])
                    else:
                        chain(nc.vector.tensor_tensor(sq[:, :, 0:NS], x1_sb[:], rows_of(u_all[:, 2, :]), ALU.mult))
                        chain(nc.vector.reduce_sum(per[:, 5, :], sq[:, :, 0:NS], AX.X))
                        chain(nc.vector.tensor_tensor(y[:, :, 0:NS], tot[:, :, 0:NS],
                                                      per[:, 5, :].unsqueeze(2).broadcast_to([P, BLK, NS]), ALU.mult))
                        chain(nc.vector.tensor_tensor(y[:, :, 0:NS], y[:, :, 0:NS], tot[:, :, NS:], ALU.add))
                        chain(nc.vector.tensor_tensor(y[:, :, 0:NS], y[:, :, 0:NS], x1_sb[:], ALU.add))
                        layernorm(y[:, :, 0:NS], y[:, :, 0:NS])
                    nc.vector.drain().then_inc(finished, 1)

        for layer in range(3):
            edge_pass(layer)
            node_stage(layer)


def kernel(x, src, dst, edge_attr_16, edge_attr_3, edge_attr_48, edge_type_90, L0_gnn_fc0_w1, L0_gnn_fc0_b1, L0_gnn_fc0_w2,
           L0_gnn_fc0_b2, L0_gnn_fc1_w1, L0_gnn_fc1_b1, L0_gnn_fc1_w2, L0_gnn_fc1_b2, L0_gnn_bn0_gs, L0_gnn_bn0_bs,
           L0_gnn_bn0_gv, L0_gnn_bn1_gs, L0_gnn_bn1_bs, L1_gnn_Ws, L1_gnn_Wa, L1_gnn_weight, L1_gnn_w_comp):
    import numpy as np
    import concourse.bacc as bacc
    from concourse.bass_utils import run_bass_kernel_spmd as run

    def tiles(a):
        return a.reshape(NT, P, *a.shape[1:]).swapaxes(0, 1)

    def groups(a):
        return a.reshape(NG, G, P).transpose(0, 2, 1)

    def second(w, b, by_output):
        w = np.concatenate([w, b[None]], 0)
        wa, wb = w[:, :NS * NS].reshape(-1, NS, NS), w[:, NS * NS:]
        if by_output:
            wb = wb.reshape(-1, NS, NV)
            return np.concatenate([wb, wa], 2).transpose(0, 2, 1).reshape(-1, W)
        wb = wb.reshape(-1, NV, NS)
        return np.concatenate([wa, wb], 1).transpose(0, 2, 1).reshape(-1, W)

    (x, src, dst, edge_attr_16, edge_attr_3, edge_attr_48, edge_type_90) = (
        np.asarray(a) for a in (x, src, dst, edge_attr_16, edge_attr_3, edge_attr_48, edge_type_90))
    f = np.asarray
    ins = {
        "x": x,
        "eaT": edge_attr_48.T,
        "heT": edge_attr_16.T,
        "ev": tiles(edge_attr_3),
        "src_row": src[None],
        "dst_row": dst[None],
        "type_row": edge_type_90[None],
        "meta": np.stack([groups(dst), groups(src)], 2),
        "w1": np.stack([f(L0_gnn_fc0_w1), f(L0_gnn_fc1_w1)], 1),
        "b1": np.stack([f(L0_gnn_fc0_b1), f(L0_gnn_fc1_b1)], 1),
        "w2": np.stack([second(f(L0_gnn_fc0_w2), f(L0_gnn_fc0_b2), True), second(f(L0_gnn_fc1_w2), f(L0_gnn_fc1_b2), False)], 1),
        "bn0": np.concatenate([f(L0_gnn_bn0_gs), f(L0_gnn_bn0_bs), f(L0_gnn_bn0_gv)])[None],
        "bn1": np.concatenate([f(L0_gnn_bn1_gs), f(L0_gnn_bn1_bs)])[None],
        "ws": f(L1_gnn_Ws),
        "wa": f(L1_gnn_Wa).reshape(3, NS).T,
        "basis": f(L1_gnn_weight).reshape(NS, NB, NS).transpose(1, 0, 2).reshape(NB, NS * NS),
        "comp": f(L1_gnn_w_comp).T,
    }
    ins = {k: np.ascontiguousarray(v) for k, v in ins.items()}
    nc = bacc.Bacc("TRN2", target_bir_lowering=False, num_devices=1)
    args = {k: nc.dram_tensor(k, v.shape, mybir.dt.from_np(v.dtype), kind="ExternalInput").ap() for k, v in ins.items()}
    out = nc.dram_tensor("out", (N, NS), FP32, kind="ExternalOutput").ap()
    build(nc, out=out, **args)
    return run(nc, [ins], core_ids=[0]).results[0]["out"]
```

```python
from contextlib import ExitStack

import concourse.bass as bass
from concourse import mybir

FP32 = mybir.dt.float32
BF16 = mybir.dt.bfloat16
U16 = mybir.dt.uint16
I32 = mybir.dt.int32
ALU = mybir.AluOpType
ACT = mybir.ActivationFunctionType
AX = mybir.AxisListType

P = 128
N = 12500
E = 400000
NT = E // P
G = 5
U = 5
GE = G * P
NG = NT // G
TURNS = NG // U
NS, NV = 16, 4
DE = 3 * NS
DH = 2 * DE
J = NS + NV
W = NS * J
R, NB = 90, 30
BLK = (N + P - 1) // P
NPAD = BLK * P
LAST = N - (BLK - 1) * P
ROWS = NPAD + P
F0, F1 = 32, 16
EPS = 1e-5
BATCHES = [(0, 2), (2, 5)]
BANK = 512
BATCH = 14
ROWS_AT = GE // 2
LATE = 3


def need(eng, sem, value):
    if isinstance(value, int) and value <= 0:
        return
    eng.wait_ge(sem, value)


def pipelined(eng, steps):
    peeled = 1 + any(lag for lag, _ in steps)
    def turn_of(it):
        for u in range(U):
            for lag, step in steps:
                turn, slot = it + (u - lag) // U, (u - lag) % U
                if isinstance(turn, int) and turn < 0:
                    continue
                step(turn, slot)
    for it in range(peeled):
        turn_of(it)
    with eng.Fori(peeled, TURNS) as it:
        turn_of(it)
    for u in range(max(lag for lag, _ in steps)):
        for lag, step in steps:
            if lag > u:
                step(TURNS + (u - lag) // U, (u - lag) % U)


def build(nc, x, eaT, he, ev, indices, dst_cols, dst_first, meta, w1, b1, w2, bn0, bn1, ws, wa, basis, comp, out):
    ctx = ExitStack()
    with ctx:
        def sb(name, shape, dt=FP32, on=ctx):
            return on.enter_context(nc.sbuf_tensor(name, shape, dt))

        def ps(name, shape, on=ctx):
            return on.enter_context(nc.psum_tensor(name, shape, FP32))

        def sem(name, on=ctx):
            return on.enter_context(nc.semaphore(name))

        def dram(name, shape, dt=FP32):
            return nc.dram_tensor(name, shape, dt, kind="Internal").ap()

        acc0 = [dram(f"acc0_{g}", [ROWS, F0]) for g in range(G)]
        acc1 = [dram(f"acc1_{g}", [ROWS, F1]) for g in range(G)]
        acc2 = [dram(f"acc2_{g}", [ROWS, F0]) for g in range(G)]
        x_tab = dram("x_tab", [ROWS, NS])
        sv_tab = dram("sv_tab", [ROWS, F0])
        x_parts = dram("x_parts", [ROWS, 3 * NS], BF16)
        sv_parts = dram("sv_parts", [ROWS, 3 * F0], BF16)
        short = dram("short", [3, E], U16)
        hidden1 = dram("hidden1", [DE, E])
        x1_tab = dram("x1_tab", [NPAD, NS])
        rel_flat = dram("rel_flat", [R * NS * NS])

        ones = sb("ones", [P, P])
        upper = sb("upper", [P, P])
        spare = sb("spare", [P, 1])
        spare_i = sb("spare_i", [P, 1], I32)
        lane = sb("lane", [P, 1])
        lane_i = sb("lane_i", [P, 1], I32)
        diff_i = sb("diff_i", [P, P], I32)
        places_i = sb("places_i", [P, P], I32)
        places = sb("places", [P, P])
        eye = sb("eye", [F0, F0])
        mask = sb("mask", [P, BLK])
        node_i = sb("node_i", [P, BLK], I32)
        w1_sb = sb("w1_sb", [P, DH])
        b1_sb = sb("b1_sb", [DH, 1])
        w2_sb = sb("w2_sb", [P, 2, W])
        bn0_sb = sb("bn0_sb", [P, 2 * NS + NV])
        bn1_sb = sb("bn1_sb", [P, 2 * NS])
        ws_sb = sb("ws_sb", [NS, NS])
        wa_sb = sb("wa_sb", [NS, 3])
        wa_rep = sb("wa_rep", [NS, 3, P])
        u_all = sb("u_all", [P, 3, NS])
        rel_parts = sb("rel_parts", [P, 3, (NS + 1) * NS], BF16)
        rhat = sb("rhat", [P, NT, 3])
        x_sb = sb("x_sb", [P, BLK, NS])
        x1_sb = sb("x1_sb", [P, BLK, NS])
        inv_count = sb("inv_count", [P, BLK])
        first = sb("first", [P, NG], I32)
        minus_node = sb("minus_node", [P, NG])
        from_first = sb("from_first", [P, NT])
        dest_all = sb("dest_all", [P, NT], I32)
        outside = sb("outside", [P, 1], I32)

        def split_rows(chain, src, parts, rest):
            chain(nc.vector.tensor_copy(parts[:, :, 0, :], src))
            chain(nc.vector.tensor_tensor(rest[0], src, parts[:, :, 0, :], ALU.subtract))
            chain(nc.vector.tensor_copy(parts[:, :, 1, :], rest[0]))
            chain(nc.vector.tensor_tensor(rest[1], rest[0], parts[:, :, 1, :], ALU.subtract))
            chain(nc.vector.tensor_copy(parts[:, :, 2, :], rest[1]))

        with ExitStack() as st:
            zeros = sb("zeros", [P, 2 * ROWS * F0 // P // 2], on=st)
            basis_sb = sb("basis_sb", [NB, NS * NS], on=st)
            comp_sb = sb("comp_sb", [NB, R], on=st)
            rel_p = sb("rel_p", [R, NS * NS], on=st)
            rel_io = sb("rel_io", [R, NS, NS], on=st)
            rel_oi = sb("rel_oi", [R, NS + 1, NS], on=st)
            rest = sb("rest", [R, 2, (NS + 1) * NS], on=st)
            ev_sb = sb("ev_sb", [P, NT, 3], on=st)
            len2 = sb("len2", [P, NT], on=st)
            work = sb("work", [P, 2 * NT], on=st)
            root, inv = work[:, 0:NT], work[:, NT:]
            away = len2
            long_sb = rhat[:].rearrange("p t k -> p (t k)").rearrange("p (k t) -> p k t", k=3).bitcast(I32)
            short_sb = sb("short_sb", [P, 3, NT], U16, on=st)
            x_split = dest_all[:, 0:BLK * 3 * NS // 2].bitcast(BF16).rearrange("p (b k f) -> p b k f", k=3, f=NS)
            x_rest = [x1_sb[:], root[:, 0:BLK * NS].rearrange("p (b f) -> p b f", f=NS)]
            long_in = sem("long_in", st)
            shortened = sem("shortened", st)
            short_out = sem("short_out", st)
            split = sem("split", st)
            ps_rel = ps("ps_rel", [R, NS * NS], on=st)
            ps_u = ps("ps_u", [P, 3, NS], on=st)
            ps_out = ps("ps_out", [P, 1], on=st)
            dst_sb = inv.bitcast(I32)
            n_out = sb("n_out", [P, 3], on=st)
            counted = sem("counted", st)
            out_total = sem("out_total", st)
            x_out = sem("x_out", st)
            loaded = sem("loaded", st)
            ev_in = sem("ev_in", st)
            iotas = sem("iotas", st)
            zeroed = sem("zeroed", st)
            cleared = sem("cleared", st)
            wa_ready = sem("wa_ready", st)
            products = sem("products", st)
            rel_copied = sem("rel_copied", st)
            rel_out = sem("rel_out", st)
            rel_in = sem("rel_in", st)
            squared = sem("squared", st)
            rooted = sem("rooted", st)
            step = sem("step", st)
            block = st.enter_context(nc.Block())
            n_loads = [0]

            @block.sync
            def _(sp):
                def load(dst, src):
                    sp.dma_start(dst, src).then_inc(loaded, 16)
                    n_loads[0] += 1
                for k in range(3):
                    sp.dma_start(long_sb[:, k, :], indices[k:k + 1, :].rearrange("a (p c) -> (a p) c", p=P)).then_inc(long_in, 16)
                sp.dma_start(ev_sb[:], ev).then_inc(ev_in, 16)
                load(w1_sb[:], w1)
                load(b1_sb[:], b1)
                load(w2_sb[:], w2)
                load(bn0_sb[:], bn0.partition_broadcast(P))
                load(bn1_sb[:], bn1.partition_broadcast(P))
                load(ws_sb[:], ws)
                load(wa_sb[:], wa)
                load(basis_sb[:], basis)
                load(comp_sb[:], comp)
                load(x_sb[:, 0:BLK - 1, :], x[0:(BLK - 1) * P, :].rearrange("(b p) f -> p b f", p=P))
                sp.wait_ge(zeroed, 2)
                load(x_sb[0:LAST, BLK - 1, :], x[(BLK - 1) * P:N, :])
                load(first[:], dst_first.partition_broadcast(P))
                load(dst_sb, dst_cols)
                sp.wait_ge(shortened, 1)
                for k in range(3):
                    sp.dma_start(short[k:k + 1, :].rearrange("a (p c) -> (a p) c", p=P), short_sb[:, k, :]).then_inc(short_out, 16)
                for a in acc0 + acc1 + acc2:
                    width = ROWS * a.shape[1] // P
                    sp.dma_start(a.rearrange("(p r) f -> p (r f)", p=P), zeros[:, 0:width]).then_inc(cleared, 16)
                sp.wait_ge(rel_copied, 1)
                sp.dma_start(rel_flat.rearrange("(i r o) -> r i o", i=NS, r=R),
                             rel_p[:].rearrange("r (i o) -> r i o", i=NS)).then_inc(rel_out, 16)
                sp.wait_ge(rel_out, 16)
                sp.dma_start(rel_io[:], rel_flat.rearrange("(r i o) -> r i o", r=R, i=NS)).then_inc(rel_in, 16)
                sp.wait_ge(loaded, 16 * n_loads[0])
                sp.dma_start(x_tab[0:NPAD, :].rearrange("(b p) f -> p b f", p=P), x_sb[:]).then_inc(x_out, 16)
                sp.dma_start(x_tab[NPAD:ROWS, :], zeros[:, 0:NS]).then_inc(x_out, 16)
                sp.dma_start(sv_tab[NPAD:ROWS, :], zeros[:, 0:F0]).then_inc(x_out, 16)
                sp.wait_ge(cleared, 16 * 3 * G)
                sp.wait_ge(split, 1)
                sp.dma_start(x_parts[0:NPAD, :].rearrange("(b p) f -> p b f", p=P),
                             x_split.rearrange("p b k f -> p b (k f)")).then_inc(x_out, 16)
                no_parts = zeros[:, 0:3 * F0 // 2].bitcast(BF16)
                sp.dma_start(x_parts[NPAD:ROWS, :], no_parts[:, 0:3 * NS]).then_inc(x_out, 16)
                sp.dma_start(sv_parts[NPAD:ROWS, :], no_parts).then_inc(x_out, 16)
                sp.wait_ge(short_out, 16 * 3)
                sp.wait_ge(x_out, 16 * 6)

            @block.gpsimd
            def _(pool):
                nc.gpsimd.iota(diff_i[:], pattern=[[1, P]], base=0, channel_multiplier=-1)
                nc.gpsimd.iota(places_i[:], pattern=[[1, P]], base=0, channel_multiplier=0)
                nc.gpsimd.iota(lane_i[:], pattern=[[0, 1]], base=0, channel_multiplier=1)
                nc.gpsimd.iota(spare_i[:], pattern=[[0, 1]], base=NPAD, channel_multiplier=1)
                nc.gpsimd.iota(node_i[:], pattern=[[P, BLK]], base=0, channel_multiplier=1).then_inc(iotas, 1)

            @block.vector
            def _(dve):
                done = [0]

                def chain(ins):
                    ins.then_inc(step, 1)
                    done[0] += 1
                    dve.wait_ge(step, done[0])
                nc.vector.memset(zeros[:], 0.0).then_inc(zeroed, 1)
                nc.vector.memset(x_sb[:, BLK - 1, :], 0.0).then_inc(zeroed, 1)
                nc.vector.memset(ones[:], 1.0)
                nc.vector.memset(rel_parts[:], 0.0)
                dve.wait_ge(iotas, 1)
                nc.vector.tensor_scalar(upper[:], diff_i[:], 0.0, None, ALU.is_ge)
                nc.vector.tensor_copy(lane[:], lane_i[:])
                nc.vector.tensor_copy(places[:], places_i[:])
                nc.vector.tensor_scalar(eye[:], diff_i[0:F0, 0:F0], 0.0, None, ALU.is_equal)
                dve.wait_ge(long_in, 16 * 3)
                nc.vector.tensor_copy(short_sb[:], long_sb).then_inc(shortened, 1)
                nc.vector.tensor_copy(spare[:], spare_i[:])
                nc.vector.tensor_scalar(mask[:], node_i[:], float(N), None, ALU.is_lt)
                dve.wait_ge(loaded, 16 * n_loads[0])
                nc.vector.tensor_copy(wa_rep[:], wa_sb[:, :].unsqueeze(2).broadcast_to([NS, 3, P])).then_inc(wa_ready, 1)
                split_rows(chain, x_sb[:], x_split, x_rest)
                nc.vector.drain().then_inc(split, 1)
                by_group = lambda a: a.rearrange("p (n g) -> p n g", g=G)
                chain(nc.vector.tensor_tensor(by_group(from_first[:]), by_group(dst_sb),
                                              first[:, :].unsqueeze(2).broadcast_to([P, NG, G]), ALU.subtract))
                nc.vector.tensor_scalar(minus_node[:], first[:], lane[:], -1.0, ALU.add, ALU.mult)
                chain(nc.vector.tensor_scalar(away[:], from_first[:], 0.0, None, ALU.is_lt))
                chain(nc.vector.reduce_sum(n_out[:, 0:1], away[:], AX.X))
                chain(nc.vector.tensor_scalar(away[:], from_first[:], float(P - 1), None, ALU.is_gt))
                chain(nc.vector.reduce_sum(n_out[:, 1:2], away[:], AX.X))
                nc.vector.tensor_tensor(n_out[:, 2:3], n_out[:, 0:1], n_out[:, 1:2], ALU.add).then_inc(counted, 1)
                dve.wait_ge(out_total, 1)
                nc.vector.tensor_copy(outside[:], ps_out[:])
                dve.wait_ge(ev_in, 16)
                chain(nc.vector.tensor_tensor(rhat[:], ev_sb[:], ev_sb[:], ALU.mult))
                nc.vector.reduce_sum(len2[:], rhat[:], AX.X).then_inc(squared, 1)
                dve.wait_ge(products, 1)
                nc.vector.tensor_copy(rel_p[:], ps_rel[:]).then_inc(rel_copied, 1)
                chain(nc.vector.tensor_copy(u_all[:], ps_u[:]))
                dve.wait_ge(rooted, 1)
                chain(nc.vector.tensor_scalar(inv, root, 1e-30, None, ALU.add))
                chain(nc.vector.reciprocal(inv, inv))
                chain(nc.vector.tensor_tensor(inv, inv, len2[:], ALU.mult))
                chain(nc.vector.tensor_tensor(root, root, inv, ALU.add))
                chain(nc.vector.tensor_scalar(root, root, 0.5, 1e-12, ALU.mult, ALU.add))
                chain(nc.vector.reciprocal(inv, root))
                nc.vector.tensor_tensor(rhat[:], ev_sb[:], inv.unsqueeze(2).broadcast_to([P, NT, 3]), ALU.mult)
                dve.wait_ge(rel_in, 16)
                nc.vector.tensor_copy(rel_oi[:, 1:, :], rel_io[:].rearrange("r i o -> r o i"))
                chain(nc.vector.tensor_copy(rel_oi[:, 0, :], u_all[0:R, 0, :]))
                flat = rel_oi[:].rearrange("r o i -> r (o i)")
                chain(nc.vector.tensor_copy(rel_parts[0:R, 0, :], flat))
                chain(nc.vector.tensor_tensor(rest[:, 0, :], flat, rel_parts[0:R, 0, :], ALU.subtract))
                chain(nc.vector.tensor_copy(rel_parts[0:R, 1, :], rest[:, 0, :]))
                chain(nc.vector.tensor_tensor(rest[:, 1, :], rest[:, 0, :], rel_parts[0:R, 1, :], ALU.subtract))
                chain(nc.vector.tensor_copy(rel_parts[0:R, 2, :], rest[:, 1, :]))

            @block.scalar
            def _(act):
                act.wait_ge(squared, 1)
                nc.scalar.activation(root, len2[:], ACT.Sqrt).then_inc(rooted, 1)

            @block.tensor
            def _(pe):
                pe.wait_ge(wa_ready, 1)
                nc.tensor.matmul(ps_rel[:], comp_sb[:], basis_sb[:], start=True, stop=True)
                for k in range(3):
                    mm = nc.tensor.matmul(ps_u[:, k, :], wa_rep[:, k, :], ws_sb[:], start=True, stop=True)
                mm.then_inc(products, 1)
                pe.wait_ge(counted, 1)
                nc.tensor.matmul(ps_out[:], ones[:], n_out[:, 2:3], start=True, stop=True).then_inc(out_total, 1)

        def pass_semaphores(layer, st):
            named = lambda what, layers=(0, 1, 2): sem(f"{what}_{layer}", st) if layer in layers else None
            in_ready = [named(f"in_ready{u}") for u in range(U)]
            rows_ready = [named(f"rows_ready{u}") for u in range(U)]
            hidden_out = [named(f"hidden_out{u}", (0,)) for u in range(U)]
            added = [named(f"added{g}") for g in range(G)]
            preset = named("preset")
            passed = named("passed")
            hid_mm = named("hid_mm", (0,))
            hid_ready = named("hid_ready", (0, 2))
            w_done = named("w_done")
            mult_done = named("mult_done")
            same_ready = named("same_ready")
            msg_ready = named("msg_ready")
            summed = named("summed")
            sums_taken = named("sums_taken")
            dest_ready = named("dest_ready")
            last_ready = named("last_ready", (0, 2))
            offset_ready = named("offset_ready", (0, 2))
            turned = named("turned", (1, 2))
            filled = named("filled", (1, 2))
            reduced = named("reduced", (0, 2))
            att_ready = named("att_ready", (2,))
            measured = named("measured")
            reads_ready = named("reads_ready", (0, 1))
            rows_mm = named("rows_mm", (0, 1))
            rows_taken = named("rows_taken", (0, 1))
            placed = named("placed", (2,))
            turned_up = named("turned_up", (2,))
            block_taken = named("block_taken", (2,))
            table_out = named("table_out", (2,))
            return (in_ready, rows_ready, hidden_out, added, preset, passed, hid_mm, hid_ready, w_done, mult_done,
                    same_ready, msg_ready, summed, sums_taken, dest_ready, last_ready, offset_ready, turned, filled,
                    reduced, att_ready, measured, reads_ready, rows_mm, rows_taken, placed, turned_up, block_taken, table_out)

        def edge_pass(layer, windowed, semaphores):
            (in_ready, rows_ready, hidden_out, added, preset, passed, hid_mm, hid_ready, w_done, mult_done,
             same_ready, msg_ready, summed, sums_taken, dest_ready, last_ready, offset_ready, turned, filled,
             reduced, att_ready, measured, reads_ready, rows_mm, rows_taken, placed, turned_up, block_taken, table_out) = semaphores
            conv = layer < 2
            gw = (NS, F0, NS)[layer]
            table = (x_tab, sv_tab, x1_tab)[layer]
            ni, nj = ((NS, J), (J, NS), (NS, NS + 1))[layer]
            wcols = ni * nj
            fw = (F0, F1, F0)[layer]
            acc = (acc0, acc1, acc2)[layer]
            start = (4, 0, 1)[layer]
            mw = start + fw
            key, to, frm = (0, 1, 0) if conv else (1, 0, 1)
            by_window, into_window = windowed and conv, windowed and not conv
            find_dests = not into_window and layer != 1
            with ExitStack() as st:
                name = lambda s: f"{s}_{layer}{'w' if windowed else ''}"
                idx = sb(name("idx"), [P, U, 2, G], I32, on=st)
                rows = sb(name("rows"), [P, U, G, gw], on=st)
                prod = sb(name("prod"), [P, U, G, wcols], on=st)
                msg = sb(name("msg"), [P, U, G, mw], on=st)
                ps_w = ps(name("ps_w"), [P, G, BANK], on=st)
                ps_sum = ps(name("ps_sum"), [P, 3 if into_window else 1, BANK], on=st)
                if layer == 0 or by_window:
                    ps_in = ps(name("ps_in"), [P, 2 if layer == 0 else 1, BANK], on=st)
                if into_window:
                    in_window = sb(name("in_window"), [P, U, G, P], on=st)
                    table_sb = sb(name("table_sb"), [F0, NPAD + P], on=st)
                    table_rows = rhat[:].rearrange("p t k -> p (t k)")[:, 0:BLK * F0].rearrange("p (b f) -> p b f", f=F0)
                else:
                    keys = sb(name("keys"), [P, U, GE], U16, on=st)
                    same = sb(name("same"), [P, U, G, P], on=st)
                    later = sb(name("later"), [P, U, G], on=st)
                    last = sb(name("last"), [P, U, G], on=st)
                    dest = sb(name("dest"), [P, U, G], I32, on=st)
                    sums = sb(name("sums"), [P, U, G, fw], on=st)
                if windowed:
                    distance = sb(name("distance"), [P, GE], on=st)
                if by_window:
                    targets = sb(name("targets"), [P, U, GE], U16, on=st)
                    reads = sb(name("reads"), [P, U, GE], BF16, on=st)
                    window = sb(name("window"), [P, U, 3, gw], BF16, on=st)
                if conv:
                    hid = sb(name("hid"), [P, U, GE], on=st)
                    turn_prod = sb(name("turn_prod"), [P, U, G, 3 * NV], on=st)
                else:
                    types = sb(name("types"), [P, U, GE], U16, on=st)
                    onehot = sb(name("onehot"), [P, U, GE], BF16, on=st)
                    he_sb = sb(name("he_sb"), [P, U, G, NS], on=st)
                    he_prod = sb(name("he_prod"), [P, U, G, NS], on=st)
                    edge = sb(name("edge"), [P, U, G], on=st)
                    att = sb(name("att"), [P, U, G], on=st)
                if layer == 0:
                    feat = sb(name("feat"), [P, U, GE], on=st)
                block = st.enter_context(nc.Block())
                dests = 2 if layer == 0 else 1
                loads = 3 + (layer == 2) + 2 * by_window - into_window

                @block.sync
                def _(sp):
                    def load(turn, u):
                        n = turn * U + u
                        if layer == 0:
                            need(sp, hid_mm, n - U + 1)
                        if layer == 1:
                            need(sp, w_done, 2 * (n - U + 1))
                            sp.sem_inc(passed)
                        if not conv:
                            need(sp, hid_ready, n - U + 1)
                            need(sp, turned, n - U + 1)
                        if by_window:
                            need(sp, rows_mm, n - U + 1)
                        if find_dests:
                            need(sp, offset_ready, n - U + 1)
                        elif not into_window:
                            need(sp, same_ready, n - U + 1)
                        sp.sem_inc(passed)
                        if not by_window:
                            need(sp, rows_ready[u], 16 * G * turn)
                            sp.sem_inc(passed)
                        e0 = n * GE
                        sp.dma_start(idx[:, u], meta[bass.ds(n, 1)].rearrange("a p k g -> (a p) k g")).then_inc(in_ready[u], 16)
                        if layer == 0:
                            sp.dma_start(feat[0:DE, u, :], eaT[:, bass.ds(e0, GE)]).then_inc(in_ready[u], 16)
                        elif layer == 1:
                            sp.dma_start(hid[0:DE, u, :], hidden1[:, bass.ds(e0, GE)]).then_inc(in_ready[u], 16)
                        else:
                            sp.dma_start(he_sb[:, u], he[bass.ds(n, 1)].rearrange("a p g f -> (a p) g f")).then_inc(in_ready[u], 16)
                            sp.dma_start(types[:, u, :], short[2:3, bass.ds(e0, GE)].partition_broadcast(P)).then_inc(in_ready[u], 16)
                        if by_window:
                            sp.dma_start(targets[:, u, :], short[1:2, bass.ds(e0, GE)].partition_broadcast(P)).then_inc(in_ready[u], 16)
                            base = sp.value_load(first[0:1, bass.ds(n, 1)], min_val=0, max_val=N - 1)
                            sp.dma_start(window[:, u].rearrange("p k f -> p (k f)"),
                                         (x_parts, sv_parts)[layer][bass.ds(base, P), :]).then_inc(in_ready[u], 16)
                        if not into_window:
                            sp.dma_start(keys[:, u, :], short[key:key + 1, bass.ds(e0, GE)].partition_broadcast(P)).then_inc(in_ready[u], 16)

                    def store_hidden(turn, u):
                        n = turn * U + u
                        need(sp, hid_ready, n + 1)
                        sp.sem_inc(passed)
                        sp.dma_start(hidden1[:, bass.ds(n * GE, GE)], hid[DE:DH, u, :]).then_inc(hidden_out[u], 16)
                    need(sp, preset, 1)
                    pipelined(sp, [(0, load)] + ([(2, store_hidden)] if layer == 0 else []))
                    if layer == 0:
                        for u in range(U):
                            sp.wait_ge(hidden_out[u], 16 * TURNS)
                    if into_window:
                        sp.wait_ge(block_taken, BLK // BATCH)
                        sp.dma_start(acc[0][0:NPAD, :].rearrange("(b p) f -> p b f", p=P), table_rows).then_inc(table_out, 16)
                        sp.wait_ge(table_out, 16)

                @block.gpsimd
                def _(pool):
                    def gather(turn, u):
                        n = turn * U + u
                        need(pool, in_ready[u], 16 * loads * (turn + 1))
                        need(pool, mult_done, 2 * (n - U + 1))
                        pool.sem_inc(passed)
                        for g in range(G):
                            nc.gpsimd.indirect_dma_start(
                                out=rows[:, u, g, :], out_offset=None, in_=table,
                                in_offset=bass.IndirectOffsetOnAxis(ap=idx[:, u, frm, g:g + 1], axis=0),
                            ).then_inc(rows_ready[u], 16)

                    def add(turn, u):
                        n = turn * U + u
                        need(pool, sums_taken, n + 1)
                        need(pool, dest_ready, (n + 1) * dests)
                        for g in range(G):
                            need(pool, added[g], 16 * n)
                            pool.sem_inc(passed)
                            nc.gpsimd.indirect_dma_start(
                                out=acc[g], out_offset=bass.IndirectOffsetOnAxis(ap=dest[:, u, g:g + 1], axis=0),
                                in_=sums[:, u, g, :], in_offset=None, compute_op=ALU.add,
                            ).then_inc(added[g], 16)
                    pipelined(pool, ([] if by_window else [(0, gather)]) + ([] if into_window else [(5, add)]))
                    if not into_window:
                        for g in range(G):
                            pool.wait_ge(added[g], 16 * NG)

                @block.tensor
                def _(pe):
                    def hidden(turn, u):
                        n = turn * U + u
                        need(pe, in_ready[u], 16 * loads * (turn + 1))
                        need(pe, hid_ready, n)
                        if by_window:
                            need(pe, rows_taken, n)
                        pe.sem_inc(passed)
                        for c in range(2):
                            mm = nc.tensor.matmul(ps_in[0:DH, c, 0:GE // 2], w1_sb[:],
                                                  feat[:, u, c * (GE // 2):(c + 1) * (GE // 2)], start=True, stop=True)
                        mm.then_inc(hid_mm, 1)

                    def read_window(turn, u):
                        n = turn * U + u
                        need(pe, in_ready[u], 16 * loads * (turn + 1))
                        need(pe, reads_ready, n + 1)
                        need(pe, rows_taken, n)
                        for g in range(G):
                            for k in range(3):
                                mm = nc.tensor.matmul(ps_in[:, 0, ROWS_AT + g * gw:ROWS_AT + (g + 1) * gw],
                                                      reads[:, u, g * P:(g + 1) * P], window[:, u, k, :], start=k == 0, stop=k == 2)
                        mm.then_inc(rows_mm, 1)

                    def weights(turn, u, g):
                        n = turn * U + u
                        if g == 0:
                            if layer == 1:
                                need(pe, in_ready[u], 16 * loads * (turn + 1))
                            else:
                                need(pe, hid_ready, n + 1)
                        for b, (g0, g1) in enumerate(BATCHES):
                            if g == g0:
                                need(pe, mult_done, 2 * n - 1 + b)
                        if conv:
                            mm = nc.tensor.matmul(ps_w[:, g, 0:wcols], hid[:, u, g * P:(g + 1) * P], w2_sb[:, layer, :],
                                                  start=True, stop=True)
                        else:
                            for k in range(3):
                                mm = nc.tensor.matmul(ps_w[:, g, 0:wcols], onehot[:, u, g * P:(g + 1) * P],
                                                      rel_parts[:, k, :], start=k == 0, stop=k == 2)
                        if any(g == g1 - 1 for _, g1 in BATCHES):
                            mm.then_inc(w_done, 1)

                    def sum_messages(turn, u, g):
                        n = turn * U + u
                        if g == 0:
                            need(pe, msg_ready, n + 1)
                            need(pe, same_ready, n + 1)
                            if into_window:
                                need(pe, placed, n - 1)
                            else:
                                need(pe, sums_taken, n)
                        if into_window:
                            mm = nc.tensor.matmul(ps_sum[0:fw, u % 3, 0:P], msg[:, u, g, start:start + fw], in_window[:, u, g, :],
                                                  start=g == 0, stop=g == G - 1)
                        else:
                            mm = nc.tensor.matmul(ps_sum[:, 0, g * fw:(g + 1) * fw], same[:, u, g, :],
                                                  msg[:, u, g, start:start + fw], start=True, stop=True)
                        if g == G - 1:
                            mm.then_inc(summed, 1)

                    def turn_and_sum(turn, u):
                        before, slot = turn + (u - LATE) // U, (u - LATE) % U
                        for g in range(G):
                            if not (isinstance(turn, int) and turn >= TURNS):
                                weights(turn, u, g)
                            if not (isinstance(before, int) and before < 0):
                                sum_messages(before, slot, g)

                    need(pe, preset, 1)
                    pipelined(pe, ([(0, hidden)] if layer == 0 else []) + ([(0, read_window)] if by_window else [])
                              + [(1, turn_and_sum)])
                    for u in range(LATE):
                        turn_and_sum(TURNS, u)
                    if into_window:
                        for k in range(BLK // BATCH):
                            need(pe, placed, NG)
                            need(pe, block_taken, k - G + 1)
                            for m in range(BATCH):
                                b = k * BATCH + m
                                mm = nc.tensor.transpose(ps_w[:, k % G, m * F0:(m + 1) * F0], table_sb[:, b * P:(b + 1) * P], eye[:])
                            mm.then_inc(turned_up, 1)

                @block.scalar
                def _(act):
                    def find_reads(turn, u):
                        n = turn * U + u
                        need(act, in_ready[u], 16 * loads * (turn + 1))
                        need(act, reads_ready, n)
                        nc.scalar.activation(distance[:], targets[:, u, :], ACT.Abs,
                                             bias=minus_node[:, bass.ds(n, 1)]).then_inc(measured, 1)
                        need(act, measured, n + 1)
                        need(act, rows_mm, n - U + 1)
                        nc.scalar.activation(reads[:, u, :], distance[:], ACT.Relu, bias=ones[:, 0:1],
                                             scale=-1.0).then_inc(reads_ready, 1)

                    def find_place(turn, u):
                        n = turn * U + u
                        need(act, same_ready, n)
                        for g in range(G):
                            ins = nc.scalar.activation(distance[:, g * P:(g + 1) * P], places[:], ACT.Abs,
                                                       bias=from_first[:, bass.ds(n * G + g, 1)], scale=-1.0)
                        ins.then_inc(measured, 1)
                        need(act, measured, n + 1)
                        need(act, summed, n - U + 1)
                        nc.scalar.activation(in_window[:, u].rearrange("p g r -> p (g r)"), distance[:], ACT.Relu,
                                             bias=ones[:, 0:1], scale=-1.0).then_inc(same_ready, 1)

                    def relu(turn, u):
                        n = turn * U + u
                        need(act, hid_mm, n + 1)
                        if by_window:
                            need(act, rows_mm, n + 1)
                        need(act, w_done, 2 * (n - U + 1))
                        need(act, hidden_out[u], 16 * turn)
                        nc.scalar.activation(hid[0:DH, u, :].rearrange("p (c e) -> p c e", c=2), ps_in[0:DH, :, 0:GE // 2],
                                             ACT.Relu, bias=b1_sb[:]).then_inc(hid_ready, 1)

                    def take_rows(turn, u):
                        n = turn * U + u
                        need(act, rows_mm, n + 1)
                        need(act, mult_done, 2 * (n - U + 1))
                        nc.scalar.activation(rows[:, u].rearrange("p g f -> p (g f)"), ps_in[:, 0, ROWS_AT:ROWS_AT + G * gw],
                                             ACT.Copy).then_inc(rows_taken, 1)

                    def take_sums(turn, u):
                        n = turn * U + u
                        need(act, summed, n + 1)
                        for g in range(G):
                            need(act, added[g], 16 * (n - U + 1))
                        nc.scalar.activation(sums[:, u].rearrange("p g f -> p (g f)"), ps_sum[:, 0, 0:G * fw],
                                             ACT.Copy).then_inc(sums_taken, 1)
                        if find_dests:
                            need(act, offset_ready, n + 1)
                            nc.scalar.activation(dest[:, u, :], later[:, u, :], ACT.Identity, bias=spare[:]).then_inc(dest_ready, 1)
                        if layer == 0:
                            nc.scalar.activation(dest_all[:, bass.ds(n * G, G)], later[:, u, :], ACT.Identity,
                                                 bias=spare[:]).then_inc(dest_ready, 1)
                        if layer == 1:
                            nc.scalar.activation(dest[:, u, :], dest_all[:, bass.ds(n * G, G)], ACT.Copy).then_inc(dest_ready, 1)
                    need(act, preset, 1)
                    if into_window:
                        pipelined(act, [(0, find_place)])
                    else:
                        pipelined(act, ([(0, find_reads)] if by_window else []) + [(5, take_sums)]
                                  + ([(0, relu)] if layer == 0 else []) + ([(0, take_rows)] if by_window else []))

                @block.vector
                def _(dve):
                    if conv:
                        nc.vector.memset(hid[0:DH, :, :], 0.0)
                        nc.vector.memset(hid[DH:P, :, :], 1.0)
                    if layer == 0:
                        nc.vector.memset(feat[:], 0.0)
                        nc.vector.memset(msg[:, :, :, J + 3 * NV:J + 3 * NV + 1], 1.0)
                        nc.vector.memset(msg[:, :, :, J + 3 * NV + 1:], 0.0)
                    if into_window:
                        nc.vector.memset(table_sb[:], 0.0)
                    nc.vector.drain().then_inc(preset, 1)
                    need(dve, preset, 1)

                    def find_same(turn, u):
                        n = turn * U + u
                        need(dve, in_ready[u], 16 * loads * (turn + 1))
                        need(dve, summed, n - U + 1)
                        if find_dests:
                            need(dve, dest_ready, (n - U + 1) * dests)
                            for g in range(G):
                                ins = nc.vector.scalar_tensor_tensor(
                                    out=same[:, u, g, :], in0=keys[:, u, g * P:(g + 1) * P], scalar=idx[:, u, to, g:g + 1],
                                    in1=upper[:], op0=ALU.is_equal, op1=ALU.mult, accum_out=later[:, u, g:g + 1])
                        else:
                            ins = nc.vector.tensor_tensor(same[:, u], keys[:, u, :].rearrange("p (g e) -> p g e", g=G),
                                                          idx[:, u, to, :].unsqueeze(2).broadcast_to([P, G, P]), ALU.is_equal)
                        ins.then_inc(same_ready, 1)

                    def find_last(turn, u):
                        n = turn * U + u
                        need(dve, same_ready, n + 1)
                        nc.vector.tensor_scalar(last[:, u, :], later[:, u, :], 1.0, None, ALU.is_equal).then_inc(last_ready, 1)

                    def find_offset(turn, u):
                        n = turn * U + u
                        need(dve, last_ready, n + 1)
                        nc.vector.scalar_tensor_tensor(out=later[:, u, :], in0=idx[:, u, to, :], scalar=spare[:], in1=last[:, u, :],
                                                       op0=ALU.subtract, op1=ALU.mult).then_inc(offset_ready, 1)

                    def place(turn, u):
                        n = turn * U + u
                        base = dve.value_load(first[0:1, bass.ds(n, 1)], min_val=0, max_val=N - 1)
                        part = table_sb[:, bass.ds(base, P)]
                        need(dve, placed, n)
                        need(dve, summed, n + 1)
                        nc.vector.tensor_tensor(part, ps_sum[0:fw, u % 3, 0:P], part, ALU.add).then_inc(placed, 1)

                    def find_type(turn, u):
                        n = turn * U + u
                        need(dve, in_ready[u], 16 * loads * (turn + 1))
                        need(dve, w_done, 2 * (n - U + 1))
                        nc.vector.tensor_scalar(onehot[:, u, :], types[:, u, :], lane[:], None,
                                                ALU.is_equal).then_inc(hid_ready, 1)

                    def edge_products(turn, u):
                        nc.vector.tensor_tensor(he_prod[:, u], he_sb[:, u],
                                                u_all[:, 1:2, :].broadcast_to([P, G, NS]), ALU.mult).then_inc(turned, 1)

                    def edge_sums(turn, u):
                        need(dve, turned, turn * U + u + 1)
                        nc.vector.reduce_sum(edge[:, u, :], he_prod[:, u], AX.X).then_inc(filled, 1)

                    def rows_here(turn, u):
                        n = turn * U + u
                        if by_window:
                            need(dve, rows_taken, n + 1)
                        else:
                            need(dve, rows_ready[u], 16 * G * (turn + 1))

                    def directions(n):
                        return rhat[:, bass.ds(n * G, G), :].unsqueeze(2).broadcast_to([P, G, NV, 3])

                    def along_products(turn, u):
                        n = turn * U + u
                        rows_here(turn, u)
                        nc.vector.tensor_tensor(turn_prod[:, u].rearrange("p g (k c) -> p g k c", c=3),
                                                rows[:, u, :, J:F0].rearrange("p g (k c) -> p g k c", c=3),
                                                directions(n), ALU.mult).then_inc(turned, 1)

                    def along_sums(turn, u):
                        need(dve, turned, turn * U + u + 1)
                        nc.vector.reduce_sum(rows[:, u, :, NS:J], turn_prod[:, u].rearrange("p g (k c) -> p g k c", c=3),
                                             AX.X).then_inc(filled, 1)

                    def multiply(turn, u, b):
                        n = turn * U + u
                        g0, g1 = BATCHES[b]
                        if b == 0:
                            rows_here(turn, u)
                            if layer == 1:
                                need(dve, filled, n + 1)
                        need(dve, w_done, 2 * n + 1 + b)
                        nc.vector.tensor_tensor(
                            prod[:, u, g0:g1, :].rearrange("p g (j i) -> p g j i", i=ni),
                            ps_w[:, g0:g1, 0:wcols].rearrange("p g (j i) -> p g j i", i=ni),
                            rows[:, u, g0:g1, 0:ni].unsqueeze(2).broadcast_to([P, g1 - g0, nj, ni]),
                            ALU.mult).then_inc(mult_done, 1)

                    def multiply_first(turn, u):
                        multiply(turn, u, 0)

                    def multiply_second(turn, u):
                        multiply(turn, u, 1)

                    def reduce(turn, u):
                        n = turn * U + u
                        need(dve, mult_done, 2 * (n + 1))
                        need(dve, summed, n - U + 1)
                        nc.vector.reduce_sum(msg[:, u, :, 0:nj], prod[:, u].rearrange("p g (j i) -> p g j i", i=ni),
                                             AX.X).then_inc(msg_ready if layer == 1 else reduced, 1)

                    def vectors(turn, u):
                        n = turn * U + u
                        need(dve, reduced, n + 1)
                        nc.vector.tensor_tensor(msg[:, u, :, J:J + 3 * NV].rearrange("p g (k c) -> p g k c", c=3),
                                                msg[:, u, :, 0:NV].unsqueeze(3).broadcast_to([P, G, NV, 3]),
                                                directions(n), ALU.mult).then_inc(msg_ready, 1)

                    def attention(turn, u):
                        n = turn * U + u
                        need(dve, reduced, n + 1)
                        need(dve, filled, n + 1)
                        nc.vector.tensor_tensor(att[:, u, :], msg[:, u, :, 0], edge[:, u, :], ALU.add).then_inc(att_ready, 1)

                    def attend(turn, u):
                        n = turn * U + u
                        need(dve, att_ready, n + 1)
                        nc.vector.tensor_tensor(msg[:, u, :, nj:], msg[:, u, :, 1:nj],
                                                att[:, u, :].unsqueeze(2).broadcast_to([P, G, NS]),
                                                ALU.mult).then_inc(msg_ready, 1)

                    if layer == 0:
                        pipelined(dve, [(0, find_same), (2, vectors), (0, multiply_first), (0, find_last), (0, multiply_second),
                                        (0, find_offset), (1, reduce)])
                    elif layer == 1:
                        pipelined(dve, [(0, along_products), (0, find_same), (0, along_sums), (1, reduce),
                                        (0, multiply_first), (0, multiply_second)])
                    else:
                        pipelined(dve, [(0, find_type), (1, edge_products)] + ([] if into_window else [(1, find_same)])
                                  + [(1, edge_sums)] + ([(5, place)] if into_window else []) + [(3, attend), (1, multiply_first)]
                                  + ([] if into_window else [(1, find_last)]) + [(1, multiply_second)]
                                  + ([] if into_window else [(1, find_offset)]) + [(2, reduce), (2, attention)])
                    if into_window:
                        for k in range(BLK // BATCH):
                            need(dve, turned_up, k + 1)
                            nc.vector.tensor_copy(table_rows[:, k * BATCH:(k + 1) * BATCH, :].rearrange("p b f -> p (b f)"),
                                                  ps_w[:, k % G, 0:BATCH * F0]).then_inc(block_taken, 1)

        def node_stage(layer):
            fw = (F0, F1, F0)[layer]
            acc = (acc0, acc1, acc2)[layer]
            with ExitStack() as st:
                name = lambda s: f"{s}_n{layer}"
                parts = sb(name("parts"), [P, G, BLK, fw], on=st)
                tot = sb(name("tot"), [P, BLK, fw], on=st)
                y = sb(name("y"), [P, BLK, F0], on=st)
                sq = sb(name("sq"), [P, BLK, F0], on=st)
                row = sb(name("row"), [P, 4, F0], on=st)
                per = sb(name("per"), [P, 6, BLK], on=st)
                ps_t = ps(name("ps_t"), [P, 2, BANK], on=st)
                in_ready = sem(name("in_ready"), st)
                partial = sem(name("partial"), st)
                total = sem(name("total"), st)
                square = sem(name("square"), st)
                rooted = sem(name("rooted"), st)
                step = sem(name("step"), st)
                stored = sem(name("stored"), st)
                finished = sem(name("finished"), st)
                n_tot = (2, 2, 0)[layer]
                roots = (1, 2, 1)[layer]
                block = st.enter_context(nc.Block())
                ncol = J if layer == 0 else NS
                if layer == 0:
                    sv_split = (parts[:, 2:4].rearrange("p g b f -> p (g b f)")[:, 0:BLK * 3 * F0 // 2].bitcast(BF16)
                                .rearrange("p (b k f) -> p b k f", k=3, f=F0))
                of_columns = (row[:, 1, 0:ncol], row[:, 2, 0:ncol])
                of_nodes = (per[:, 1, :], per[:, 2, :])
                rounds = ([of_columns], [of_columns, of_nodes], [of_nodes])[layer]

                @block.sync
                def _(sp):
                    for g in range(G):
                        sp.dma_start(parts[:, g], acc[g][0:NPAD, :].rearrange("(b p) f -> p b f", p=P)).then_inc(in_ready, 16)
                    sp.wait_ge(finished, 1)
                    if layer == 0:
                        sp.dma_start(sv_tab[0:NPAD, :].rearrange("(b p) f -> p b f", p=P), y[:]).then_inc(stored, 16)
                        sp.dma_start(sv_parts[0:NPAD, :].rearrange("(b p) f -> p b f", p=P),
                                     sv_split.rearrange("p b k f -> p b (k f)")).then_inc(stored, 16)
                        sp.wait_ge(stored, 32)
                    elif layer == 1:
                        sp.dma_start(x1_tab.rearrange("(b p) f -> p b f", p=P), x1_sb[:]).then_inc(stored, 16)
                        sp.wait_ge(stored, 16)
                    else:
                        sp.dma_start(out[0:(BLK - 1) * P, :].rearrange("(b p) f -> p b f", p=P),
                                     y[:, 0:BLK - 1, 0:NS]).then_inc(stored, 16)
                        sp.dma_start(out[(BLK - 1) * P:N, :], y[0:LAST, BLK - 1, 0:NS]).then_inc(stored, 16)
                        sp.wait_ge(stored, 32)

                @block.tensor
                def _(pe):
                    for k in range(n_tot):
                        pe.wait_ge(partial, k + 1)
                        nc.tensor.matmul(ps_t[:, k, 0:F0], ones[:], row[:, 0, :], start=True, stop=True).then_inc(total, 1)

                @block.scalar
                def _(act):
                    for k, (square_of, root_of) in enumerate(rounds):
                        act.wait_ge(square, k + 1)
                        nc.scalar.activation(root_of, square_of, ACT.Sqrt).then_inc(rooted, 1)

                @block.vector
                def _(dve):
                    done = [0]

                    def chain(ins):
                        ins.then_inc(step, 1)
                        done[0] += 1
                        dve.wait_ge(step, done[0])

                    def over_nodes(part, k):
                        nc.vector.drain().then_inc(partial, 1)
                        dve.wait_ge(total, k + 1)

                    def inverse_root(a, root, out_, spare_, k):
                        nc.vector.drain().then_inc(square, 1)
                        dve.wait_ge(rooted, k + 1)
                        chain(nc.vector.reciprocal(spare_, root))
                        chain(nc.vector.tensor_tensor(spare_, spare_, a, ALU.mult))
                        chain(nc.vector.tensor_tensor(spare_, spare_, root, ALU.add))
                        chain(nc.vector.tensor_scalar(spare_, spare_, 0.5, None, ALU.mult))
                        chain(nc.vector.reciprocal(out_, spare_))

                    def rows_of(a, n=None):
                        return a.unsqueeze(1).broadcast_to([P, BLK, a.shape[-1]])

                    def layernorm(dst, src):
                        chain(nc.vector.reduce_sum(per[:, 0, :], src, AX.X))
                        chain(nc.vector.tensor_scalar(per[:, 0, :], per[:, 0, :], 1.0 / NS, None, ALU.mult))
                        chain(nc.vector.tensor_tensor(src, src, per[:, 0, :].unsqueeze(2).broadcast_to([P, BLK, NS]), ALU.subtract))
                        chain(nc.vector.tensor_tensor(sq[:, :, 0:NS], src, src, ALU.mult))
                        chain(nc.vector.reduce_sum(per[:, 1, :], sq[:, :, 0:NS], AX.X))
                        chain(nc.vector.tensor_scalar(per[:, 1, :], per[:, 1, :], 1.0 / NS, EPS, ALU.mult, ALU.add))
                        inverse_root(per[:, 1, :], per[:, 2, :], per[:, 3, :], per[:, 4, :], roots - 1)
                        chain(nc.vector.tensor_tensor(dst, src, per[:, 3, :].unsqueeze(2).broadcast_to([P, BLK, NS]), ALU.mult))

                    dve.wait_ge(in_ready, 16 * G)
                    chain(nc.vector.tensor_tensor(tot[:], parts[:, 0], parts[:, 1], ALU.add))
                    for g in range(2, G):
                        chain(nc.vector.tensor_tensor(tot[:], tot[:], parts[:, g], ALU.add))
                    if layer < 2:
                        if layer == 0:
                            chain(nc.vector.tensor_scalar(inv_count[:], tot[:, :, NS + 3 * NV], 1.0, None, ALU.max))
                            chain(nc.vector.reciprocal(inv_count[:], inv_count[:]))
                        scale = 0.25 if layer == 0 else float((NS + NV) ** -0.5)
                        chain(nc.vector.tensor_scalar(per[:, 5, :], inv_count[:], scale, None, ALU.mult))
                        chain(nc.vector.tensor_tensor(y[:, :, 0:NS], tot[:, :, 0:NS],
                                                      per[:, 5, :].unsqueeze(2).broadcast_to([P, BLK, NS]), ALU.mult))
                        chain(nc.vector.memset(row[:], 0.0))
                        chain(nc.vector.reduce_sum(row[:, 0, 0:NS], y[:, :, 0:NS].rearrange("p b f -> p f b"), AX.X))
                        over_nodes(None, 0)
                        chain(nc.vector.tensor_scalar(row[:, 3, 0:NS], ps_t[:, 0, 0:NS], 1.0 / N, None, ALU.mult))
                        chain(nc.vector.tensor_tensor(y[:, :, 0:NS], y[:, :, 0:NS], rows_of(row[:, 3, 0:NS]), ALU.subtract))
                        chain(nc.vector.tensor_tensor(y[:, :, 0:NS], y[:, :, 0:NS],
                                                      mask[:, :].unsqueeze(2).broadcast_to([P, BLK, NS]), ALU.mult))
                        chain(nc.vector.tensor_tensor(sq[:, :, 0:NS], y[:, :, 0:NS], y[:, :, 0:NS], ALU.mult))
                        chain(nc.vector.reduce_sum(row[:, 0, 0:NS], sq[:, :, 0:NS].rearrange("p b f -> p f b"), AX.X))
                        if layer == 0:
                            chain(nc.vector.tensor_scalar(per[:, 5, :], inv_count[:], 0.25 * 3.0 ** 0.5, None, ALU.mult))
                            chain(nc.vector.tensor_tensor(y[:, :, J:F0], tot[:, :, NS:NS + 3 * NV],
                                                          per[:, 5, :].unsqueeze(2).broadcast_to([P, BLK, 3 * NV]), ALU.mult))
                            chain(nc.vector.tensor_tensor(sq[:, :, J:F0], y[:, :, J:F0], y[:, :, J:F0], ALU.mult))
                            chain(nc.vector.reduce_sum(row[:, 1, 0:3 * NV], sq[:, :, J:F0].rearrange("p b f -> p f b"), AX.X))
                            chain(nc.vector.reduce_sum(row[:, 0, NS:J], row[:, 1, 0:3 * NV].rearrange("p (k c) -> p k c", c=3), AX.X))
                        over_nodes(None, 1)
                        chain(nc.vector.tensor_scalar(row[:, 1, 0:NS], ps_t[:, 1, 0:NS], 1.0 / N, EPS, ALU.mult, ALU.add))
                        if layer == 0:
                            chain(nc.vector.tensor_scalar(row[:, 1, NS:J], ps_t[:, 1, NS:J], 1.0 / (3 * N), EPS, ALU.mult, ALU.add))
                        inverse_root(row[:, 1, 0:ncol], row[:, 2, 0:ncol], row[:, 3, 0:ncol], row[:, 0, 0:ncol], 0)
                        gains = bn0_sb if layer == 0 else bn1_sb
                        chain(nc.vector.tensor_tensor(row[:, 0, 0:NS], row[:, 3, 0:NS], gains[:, 0:NS], ALU.mult))
                        chain(nc.vector.tensor_tensor(y[:, :, 0:NS], y[:, :, 0:NS], rows_of(row[:, 0, 0:NS]), ALU.mult))
                        chain(nc.vector.tensor_tensor(y[:, :, 0:NS], y[:, :, 0:NS], rows_of(gains[:, NS:2 * NS]), ALU.add))
                        if layer == 0:
                            chain(nc.vector.tensor_tensor(row[:, 0, NS:J], row[:, 3, NS:J], gains[:, 2 * NS:], ALU.mult))
                            chain(nc.vector.tensor_tensor(
                                y[:, :, J:F0].rearrange("p b (k c) -> p b k c", c=3), y[:, :, J:F0].rearrange("p b (k c) -> p b k c", c=3),
                                row[:, 0, NS:J].unsqueeze(1).unsqueeze(3).broadcast_to([P, BLK, NV, 3]), ALU.mult))
                            chain(nc.vector.memset(y[:, :, NS:J], 0.0))
                            split_rows(chain, y[:], sv_split, [parts[:, 0], parts[:, 1]])
                        else:
                            chain(nc.vector.tensor_tensor(y[:, :, 0:NS], y[:, :, 0:NS], x_sb[:], ALU.add))
                            layernorm(x1_sb[:], y[:, :, 0:NS])
                    else:
                        chain(nc.vector.tensor_tensor(sq[:, :, 0:NS], x1_sb[:], rows_of(u_all[:, 2, :]), ALU.mult))
                        chain(nc.vector.reduce_sum(per[:, 5, :], sq[:, :, 0:NS], AX.X))
                        chain(nc.vector.tensor_tensor(y[:, :, 0:NS], tot[:, :, 0:NS],
                                                      per[:, 5, :].unsqueeze(2).broadcast_to([P, BLK, NS]), ALU.mult))
                        chain(nc.vector.tensor_tensor(y[:, :, 0:NS], y[:, :, 0:NS], tot[:, :, NS:], ALU.add))
                        chain(nc.vector.tensor_tensor(y[:, :, 0:NS], y[:, :, 0:NS], x1_sb[:], ALU.add))
                        layernorm(y[:, :, 0:NS], y[:, :, 0:NS])
                    nc.vector.drain().then_inc(finished, 1)

        n_outside = nc.values_load(outside[0:1, 0:1], min_val=0, max_val=2 * E)
        for layer in range(3):
            with ExitStack() as st:
                semaphores = pass_semaphores(layer, st)
                with nc.If(n_outside == 0):
                    edge_pass(layer, True, semaphores)
                with nc.Else():
                    edge_pass(layer, False, semaphores)
            node_stage(layer)


def kernel(x, src, dst, edge_attr_16, edge_attr_3, edge_attr_48, edge_type_90, L0_gnn_fc0_w1, L0_gnn_fc0_b1, L0_gnn_fc0_w2,
           L0_gnn_fc0_b2, L0_gnn_fc1_w1, L0_gnn_fc1_b1, L0_gnn_fc1_w2, L0_gnn_fc1_b2, L0_gnn_bn0_gs, L0_gnn_bn0_bs,
           L0_gnn_bn0_gv, L0_gnn_bn1_gs, L0_gnn_bn1_bs, L1_gnn_Ws, L1_gnn_Wa, L1_gnn_weight, L1_gnn_w_comp):
    import numpy as np
    import concourse.bacc as bacc
    from concourse.bass_utils import run_bass_kernel_spmd as run

    def tiles(a):
        return a.reshape(NT, P, *a.shape[1:]).swapaxes(0, 1)

    def groups(a):
        return a.reshape(NG, G, P).transpose(0, 2, 1)

    def second(w, b, by_output):
        w = np.concatenate([w, np.zeros((DH - DE, W), np.float32), b[None], np.zeros((P - DH - 1, W), np.float32)], 0)
        wa, wb = w[:, :NS * NS].reshape(-1, NS, NS), w[:, NS * NS:]
        if by_output:
            wb = wb.reshape(-1, NS, NV)
            return np.concatenate([wb, wa], 2).transpose(0, 2, 1).reshape(-1, W)
        wb = wb.reshape(-1, NV, NS)
        return np.concatenate([wa, wb], 1).transpose(0, 2, 1).reshape(-1, W)

    (x, src, dst, edge_attr_16, edge_attr_3, edge_attr_48, edge_type_90) = (
        np.asarray(a) for a in (x, src, dst, edge_attr_16, edge_attr_3, edge_attr_48, edge_type_90))
    f = np.asarray
    ins = {
        "x": x,
        "eaT": edge_attr_48.T,
        "he": edge_attr_16.reshape(NG, G, P, NS).transpose(0, 2, 1, 3),
        "ev": tiles(edge_attr_3),
        "indices": np.stack([src, dst, edge_type_90]),
        "dst_cols": tiles(dst),
        "dst_first": dst[None, ::GE],
        "meta": np.stack([groups(dst), groups(src)], 2),
        "w1": np.concatenate([np.concatenate([f(L0_gnn_fc0_w1), f(L0_gnn_fc1_w1)], 1), np.zeros((P - DE, DH), np.float32)], 0),
        "b1": np.concatenate([f(L0_gnn_fc0_b1), f(L0_gnn_fc1_b1)])[:, None],
        "w2": np.stack([second(f(L0_gnn_fc0_w2), f(L0_gnn_fc0_b2), True), second(f(L0_gnn_fc1_w2), f(L0_gnn_fc1_b2), False)], 1),
        "bn0": np.concatenate([f(L0_gnn_bn0_gs), f(L0_gnn_bn0_bs), f(L0_gnn_bn0_gv)])[None],
        "bn1": np.concatenate([f(L0_gnn_bn1_gs), f(L0_gnn_bn1_bs)])[None],
        "ws": f(L1_gnn_Ws),
        "wa": f(L1_gnn_Wa).reshape(3, NS).T,
        "basis": f(L1_gnn_weight).reshape(NS, NB, NS).transpose(1, 0, 2).reshape(NB, NS * NS),
        "comp": f(L1_gnn_w_comp).T,
    }
    ins = {k: np.ascontiguousarray(v) for k, v in ins.items()}
    nc = bacc.Bacc("TRN2", target_bir_lowering=False, num_devices=1)
    args = {k: nc.dram_tensor(k, v.shape, mybir.dt.from_np(v.dtype), kind="ExternalInput").ap() for k, v in ins.items()}
    out = nc.dram_tensor("out", (N, NS), FP32, kind="ExternalOutput").ap()
    build(nc, out=out, **args)
    return run(nc, [ins], core_ids=[0]).results[0]["out"]
```

```python
from contextlib import ExitStack

import concourse.bass as bass
from concourse import mybir

FP32 = mybir.dt.float32
BF16 = mybir.dt.bfloat16
U16 = mybir.dt.uint16
I32 = mybir.dt.int32
ALU = mybir.AluOpType
ACT = mybir.ActivationFunctionType
AX = mybir.AxisListType

P = 128
N = 12500
E = 400000
NT = E // P
G = 5
U = 5
GE = G * P
NG = NT // G
TURNS = NG // U
NS, NV = 16, 4
DE = 3 * NS
DH = 2 * DE
J = NS + NV
W = NS * J
R, NB = 90, 30
BLK = (N + P - 1) // P
NPAD = BLK * P
LAST = N - (P - 1) * BLK
ROWS = NPAD + P
F0, F1 = 32, 16
EPS = 1e-5
BATCHES = [(0, 2), (2, 5)]
BANK = 512
BATCH = 14
ROWS_AT = GE // 2
LATE = 3


def need(eng, sem, value):
    if isinstance(value, int) and value <= 0:
        return
    eng.wait_ge(sem, value)


def pipelined(eng, steps):
    peeled = 1 + any(lag for lag, _ in steps)
    def turn_of(it):
        for u in range(U):
            for lag, step in steps:
                turn, slot = it + (u - lag) // U, (u - lag) % U
                if isinstance(turn, int) and turn < 0:
                    continue
                step(turn, slot)
    for it in range(peeled):
        turn_of(it)
    with eng.Fori(peeled, TURNS) as it:
        turn_of(it)
    for u in range(max(lag for lag, _ in steps)):
        for lag, step in steps:
            if lag > u:
                step(TURNS + (u - lag) // U, (u - lag) % U)


def build(nc, x, eaT, he, ev, indices, dst_cols, dst_first, meta, w1, b1, w2, bn0, bn1, ws, wa, basis, comp, out):
    ctx = ExitStack()
    with ctx:
        def sb(name, shape, dt=FP32, on=ctx):
            return on.enter_context(nc.sbuf_tensor(name, shape, dt))

        def ps(name, shape, on=ctx):
            return on.enter_context(nc.psum_tensor(name, shape, FP32))

        def sem(name, on=ctx):
            return on.enter_context(nc.semaphore(name))

        def dram(name, shape, dt=FP32):
            return nc.dram_tensor(name, shape, dt, kind="Internal").ap()

        acc0 = [dram(f"acc0_{g}", [ROWS, F0]) for g in range(G)]
        acc1 = [dram(f"acc1_{g}", [ROWS, F1]) for g in range(G)]
        acc2 = [dram(f"acc2_{g}", [ROWS, F0]) for g in range(G)]
        x_tab = dram("x_tab", [ROWS, NS])
        sv_tab = dram("sv_tab", [ROWS, F0])
        x_parts = dram("x_parts", [ROWS, 3 * NS], BF16)
        sv_parts = dram("sv_parts", [ROWS, 3 * F0], BF16)
        short = dram("short", [3, E], U16)
        hidden1 = dram("hidden1", [DE, E])
        x1_tab = dram("x1_tab", [NPAD, NS])
        rel_flat = dram("rel_flat", [R * NS * NS])

        ones = sb("ones", [P, P])
        upper = sb("upper", [P, P])
        spare = sb("spare", [P, 1])
        minus_spare = sb("minus_spare", [P, 1])
        spare_i = sb("spare_i", [P, 1], I32)
        lane = sb("lane", [P, 1])
        lane_i = sb("lane_i", [P, 1], I32)
        diff_i = sb("diff_i", [P, P], I32)
        places_i = sb("places_i", [P, P], I32)
        places = sb("places", [P, P])
        eye = sb("eye", [F0, F0])
        mask = sb("mask", [P, BLK])
        node_i = sb("node_i", [P, BLK], I32)
        w1_sb = sb("w1_sb", [P, DH])
        b1_sb = sb("b1_sb", [DH, 1])
        w2_sb = sb("w2_sb", [P, 2, W])
        bn0_sb = sb("bn0_sb", [P, 2 * NS + NV])
        bn1_sb = sb("bn1_sb", [P, 2 * NS])
        ws_sb = sb("ws_sb", [NS, NS])
        wa_sb = sb("wa_sb", [NS, 3])
        wa_rep = sb("wa_rep", [NS, 3, P])
        u_all = sb("u_all", [P, 3, NS])
        rel_parts = sb("rel_parts", [P, 3, (NS + 1) * NS], BF16)
        rhat = sb("rhat", [P, NT, 3])
        table_rows = rhat[:].rearrange("p t k -> p (t k)")[:, 0:BLK * F0].rearrange("p (b f) -> p b f", f=F0)
        x_sb = sb("x_sb", [P, BLK, NS])
        x1_all = sb("x1_all", [P, BLK + 1, NS])
        x1_sb = x1_all[:, 0:BLK, :]
        inv_count = sb("inv_count", [P, BLK])
        first = sb("first", [P, NG], I32)
        minus_node = sb("minus_node", [P, NG])
        from_first = sb("from_first", [P, NT])
        dest_all = sb("dest_all", [P, NT], I32)
        outside = sb("outside", [P, 1], I32)

        def split_rows(chain, src, parts, rest):
            chain(nc.vector.tensor_copy(parts[:, :, 0, :], src))
            chain(nc.vector.tensor_tensor(rest[0], src, parts[:, :, 0, :], ALU.subtract))
            chain(nc.vector.tensor_copy(parts[:, :, 1, :], rest[0]))
            chain(nc.vector.tensor_tensor(rest[1], rest[0], parts[:, :, 1, :], ALU.subtract))
            chain(nc.vector.tensor_copy(parts[:, :, 2, :], rest[1]))

        with ExitStack() as st:
            zeros = sb("zeros", [P, ROWS * F0 // P], on=st)
            basis_sb = sb("basis_sb", [NB, NS * NS], on=st)
            comp_sb = sb("comp_sb", [NB, R], on=st)
            rel_p = sb("rel_p", [R, NS * NS], on=st)
            rel_io = sb("rel_io", [R, NS, NS], on=st)
            rel_oi = sb("rel_oi", [R, NS + 1, NS], on=st)
            rest = sb("rest", [R, 2, (NS + 1) * NS], on=st)
            ev_sb = sb("ev_sb", [P, NT, 3], on=st)
            len2 = sb("len2", [P, NT], on=st)
            work = sb("work", [P, 2 * NT], on=st)
            root, inv = work[:, 0:NT], work[:, NT:]
            away = len2
            long_sb = rhat[:].rearrange("p t k -> p (t k)").rearrange("p (k t) -> p k t", k=3).bitcast(I32)
            short_sb = sb("short_sb", [P, 3, NT], U16, on=st)
            x_split = dest_all[:, 0:BLK * 3 * NS // 2].bitcast(BF16).rearrange("p (b k f) -> p b k f", k=3, f=NS)
            x_rest = [len2[:, 0:BLK * NS].rearrange("p (b f) -> p b f", f=NS), root[:, 0:BLK * NS].rearrange("p (b f) -> p b f", f=NS)]
            long_in = sem("long_in", st)
            shortened = sem("shortened", st)
            short_out = sem("short_out", st)
            split = sem("split", st)
            ps_rel = ps("ps_rel", [R, NS * NS], on=st)
            ps_u = ps("ps_u", [P, 3, NS], on=st)
            ps_out = ps("ps_out", [P, 1], on=st)
            dst_sb = inv.bitcast(I32)
            n_out = sb("n_out", [P, 3], on=st)
            counted = sem("counted", st)
            out_total = sem("out_total", st)
            x_out = sem("x_out", st)
            loaded = sem("loaded", st)
            ev_in = sem("ev_in", st)
            dst_in = sem("dst_in", st)
            ev_squared = sem("ev_squared", st)
            iotas = sem("iotas", st)
            zeroed = sem("zeroed", st)
            cleared = sem("cleared", st)
            wa_ready = sem("wa_ready", st)
            products = sem("products", st)
            rel_copied = sem("rel_copied", st)
            rel_out = sem("rel_out", st)
            rel_in = sem("rel_in", st)
            squared = sem("squared", st)
            rooted = sem("rooted", st)
            step = sem("step", st)
            block = st.enter_context(nc.Block())
            n_loads = [0]

            @block.sync
            def _(sp):
                def load(dst, src):
                    sp.dma_start(dst, src).then_inc(loaded, 16)
                    n_loads[0] += 1
                for k in range(3):
                    sp.dma_start(long_sb[:, k, :], indices[k:k + 1, :].rearrange("a (p c) -> (a p) c", p=P)).then_inc(long_in, 16)
                sp.dma_start(first[:], dst_first.partition_broadcast(P)).then_inc(dst_in, 16)
                sp.dma_start(dst_sb, dst_cols).then_inc(dst_in, 16)
                sp.dma_start(ev_sb[:], ev).then_inc(ev_in, 16)
                load(w1_sb[:], w1)
                load(b1_sb[:], b1)
                load(w2_sb[:], w2)
                load(bn0_sb[:], bn0.partition_broadcast(P))
                load(bn1_sb[:], bn1.partition_broadcast(P))
                load(ws_sb[:], ws)
                load(wa_sb[:], wa)
                load(basis_sb[:], basis)
                load(comp_sb[:], comp)
                sp.wait_ge(zeroed, 2)
                load(x_sb[0:P - 1], x[0:(P - 1) * BLK, :].rearrange("(p b) f -> p b f", p=P - 1))
                load(x_sb[P - 1:P, 0:LAST, :], x[(P - 1) * BLK:N, :].rearrange("(p b) f -> p b f", p=1))
                sp.wait_ge(shortened, 1)
                for k in range(3):
                    sp.dma_start(short[k:k + 1, :].rearrange("a (p c) -> (a p) c", p=P), short_sb[:, k, :]).then_inc(short_out, 16)
                for a in acc0:
                    width = ROWS * a.shape[1] // P
                    sp.dma_start(a.rearrange("(p r) f -> p (r f)", p=P), zeros[:, 0:width]).then_inc(cleared, 16)
                sp.wait_ge(rel_copied, 1)
                sp.dma_start(rel_flat.rearrange("(i r o) -> r i o", i=NS, r=R),
                             rel_p[:].rearrange("r (i o) -> r i o", i=NS)).then_inc(rel_out, 16)
                sp.wait_ge(rel_out, 16)
                sp.dma_start(rel_io[:], rel_flat.rearrange("(r i o) -> r i o", r=R, i=NS)).then_inc(rel_in, 16)
                sp.wait_ge(loaded, 16 * n_loads[0])
                sp.dma_start(x_tab[0:NPAD, :].rearrange("(p b) f -> p b f", p=P), x_sb[:]).then_inc(x_out, 16)
                sp.dma_start(x_tab[NPAD:ROWS, :], zeros[:, 0:NS]).then_inc(x_out, 16)
                sp.dma_start(sv_tab[NPAD:ROWS, :], zeros[:, 0:F0]).then_inc(x_out, 16)
                sp.wait_ge(cleared, 16 * G)
                sp.wait_ge(split, 1)
                sp.dma_start(x_parts[0:NPAD, :].rearrange("(p b) f -> p b f", p=P),
                             x_split.rearrange("p b k f -> p b (k f)")).then_inc(x_out, 16)
                no_parts = zeros[:, 0:3 * F0 // 2].bitcast(BF16)
                sp.dma_start(x_parts[NPAD:ROWS, :], no_parts[:, 0:3 * NS]).then_inc(x_out, 16)
                sp.dma_start(sv_parts[NPAD:ROWS, :], no_parts).then_inc(x_out, 16)
                sp.wait_ge(short_out, 16 * 3)
                sp.wait_ge(x_out, 16 * 6)

            @block.gpsimd
            def _(pool):
                nc.gpsimd.iota(diff_i[:], pattern=[[1, P]], base=0, channel_multiplier=-1)
                nc.gpsimd.iota(places_i[:], pattern=[[1, P]], base=0, channel_multiplier=0)
                nc.gpsimd.iota(lane_i[:], pattern=[[0, 1]], base=0, channel_multiplier=1)
                nc.gpsimd.iota(spare_i[:], pattern=[[0, 1]], base=NPAD, channel_multiplier=1)
                nc.gpsimd.iota(node_i[:], pattern=[[1, BLK]], base=0, channel_multiplier=BLK).then_inc(iotas, 1)
                pool.wait_ge(ev_in, 16)
                pool.wait_ge(shortened, 1)
                nc.gpsimd.tensor_tensor(rhat[:], ev_sb[:], ev_sb[:], ALU.mult).then_inc(ev_squared, 1)

            @block.vector
            def _(dve):
                done = [0]

                def chain(ins):
                    ins.then_inc(step, 1)
                    done[0] += 1
                    dve.wait_ge(step, done[0])
                nc.vector.memset(zeros[:], 0.0).then_inc(zeroed, 1)
                nc.vector.memset(x_sb[96:P, LAST:, :], 0.0).then_inc(zeroed, 1)
                nc.vector.memset(ones[:], 1.0)
                nc.vector.memset(rel_parts[:], 0.0)
                nc.vector.memset(x1_all[:], 0.0)
                dve.wait_ge(iotas, 1)
                nc.vector.tensor_scalar(upper[:], diff_i[:], 0.0, None, ALU.is_ge)
                nc.vector.tensor_copy(lane[:], lane_i[:])
                nc.vector.tensor_copy(places[:], places_i[:])
                nc.vector.tensor_scalar(eye[:], diff_i[0:F0, 0:F0], 0.0, None, ALU.is_equal)
                dve.wait_ge(long_in, 16 * 3)
                nc.vector.tensor_copy(short_sb[:], long_sb).then_inc(shortened, 1)
                nc.vector.tensor_copy(spare[:], spare_i[:])
                nc.vector.tensor_scalar(minus_spare[:], spare_i[:], -1.0, None, ALU.mult)
                nc.vector.tensor_scalar(mask[:], node_i[:], float(N), None, ALU.is_lt)
                dve.wait_ge(dst_in, 32)
                by_group = lambda a: a.rearrange("p (n g) -> p n g", g=G)
                chain(nc.vector.tensor_tensor(by_group(from_first[:]), by_group(dst_sb),
                                              first[:, :].unsqueeze(2).broadcast_to([P, NG, G]), ALU.subtract))
                nc.vector.tensor_scalar(minus_node[:], first[:], lane[:], -1.0, ALU.add, ALU.mult)
                chain(nc.vector.tensor_scalar(away[:], from_first[:], 0.0, None, ALU.is_lt))
                chain(nc.vector.reduce_sum(n_out[:, 0:1], away[:], AX.X))
                chain(nc.vector.tensor_scalar(away[:], from_first[:], float(P - 1), None, ALU.is_gt))
                chain(nc.vector.reduce_sum(n_out[:, 1:2], away[:], AX.X))
                nc.vector.tensor_tensor(n_out[:, 2:3], n_out[:, 0:1], n_out[:, 1:2], ALU.add).then_inc(counted, 1)
                dve.wait_ge(loaded, 16 * n_loads[0])
                nc.vector.tensor_copy(wa_rep[:], wa_sb[:, :].unsqueeze(2).broadcast_to([NS, 3, P])).then_inc(wa_ready, 1)
                split_rows(chain, x_sb[:], x_split, x_rest)
                nc.vector.drain().then_inc(split, 1)
                dve.wait_ge(out_total, 1)
                nc.vector.tensor_copy(outside[:], ps_out[:])
                dve.wait_ge(ev_in, 16)
                dve.wait_ge(ev_squared, 1)
                nc.vector.reduce_sum(len2[:], rhat[:], AX.X).then_inc(squared, 1)
                dve.wait_ge(products, 1)
                nc.vector.tensor_copy(rel_p[:], ps_rel[:]).then_inc(rel_copied, 1)
                chain(nc.vector.tensor_copy(u_all[:], ps_u[:]))
                dve.wait_ge(rooted, 1)
                chain(nc.vector.tensor_scalar(inv, root, 1e-30, None, ALU.add))
                chain(nc.vector.reciprocal(inv, inv))
                chain(nc.vector.tensor_tensor(inv, inv, len2[:], ALU.mult))
                chain(nc.vector.tensor_tensor(root, root, inv, ALU.add))
                chain(nc.vector.tensor_scalar(root, root, 0.5, 1e-12, ALU.mult, ALU.add))
                chain(nc.vector.reciprocal(inv, root))
                nc.vector.tensor_tensor(rhat[:], ev_sb[:], inv.unsqueeze(2).broadcast_to([P, NT, 3]), ALU.mult)
                dve.wait_ge(rel_in, 16)
                nc.vector.tensor_copy(rel_oi[:, 1:, :], rel_io[:].rearrange("r i o -> r o i"))
                chain(nc.vector.tensor_copy(rel_oi[:, 0, :], u_all[0:R, 0, :]))
                flat = rel_oi[:].rearrange("r o i -> r (o i)")
                chain(nc.vector.tensor_copy(rel_parts[0:R, 0, :], flat))
                chain(nc.vector.tensor_tensor(rest[:, 0, :], flat, rel_parts[0:R, 0, :], ALU.subtract))
                chain(nc.vector.tensor_copy(rel_parts[0:R, 1, :], rest[:, 0, :]))
                chain(nc.vector.tensor_tensor(rest[:, 1, :], rest[:, 0, :], rel_parts[0:R, 1, :], ALU.subtract))
                chain(nc.vector.tensor_copy(rel_parts[0:R, 2, :], rest[:, 1, :]))

            @block.scalar
            def _(act):
                act.wait_ge(squared, 1)
                nc.scalar.activation(root, len2[:], ACT.Sqrt).then_inc(rooted, 1)

            @block.tensor
            def _(pe):
                pe.wait_ge(wa_ready, 1)
                nc.tensor.matmul(ps_rel[:], comp_sb[:], basis_sb[:], start=True, stop=True)
                for k in range(3):
                    mm = nc.tensor.matmul(ps_u[:, k, :], wa_rep[:, k, :], ws_sb[:], start=True, stop=True)
                mm.then_inc(products, 1)
                pe.wait_ge(counted, 1)
                nc.tensor.matmul(ps_out[:], ones[:], n_out[:, 2:3], start=True, stop=True).then_inc(out_total, 1)

        passed = sem("passed")

        def pass_semaphores(layer, st):
            named = lambda what, layers=(0, 1, 2): sem(f"{what}_{layer}", st) if layer in layers else None
            in_ready = [named(f"in_ready{u}") for u in range(U)]
            rows_ready = [named(f"rows_ready{u}") for u in range(U)]
            hidden_out = [named(f"hidden_out{u}", (0,)) for u in range(U)]
            added = [named(f"added{g}") for g in range(G)]
            preset = named("preset")
            hid_mm = named("hid_mm", (0,))
            hid_ready = named("hid_ready", (0, 2))
            w_done = named("w_done")
            mult_done = named("mult_done")
            same_ready = named("same_ready")
            msg_ready = named("msg_ready")
            summed = named("summed")
            sums_taken = named("sums_taken")
            dest_ready = named("dest_ready")
            shifted = named("shifted", (0, 2))
            offset_ready = named("offset_ready", (0, 2))
            turned = named("turned", (1, 2))
            filled = named("filled", (1, 2))
            reduced = named("reduced", (0, 2))
            att_ready = named("att_ready", (2,))
            measured = named("measured")
            reads_ready = named("reads_ready", (0, 1))
            rows_mm = named("rows_mm", (0, 1))
            rows_taken = named("rows_taken", (0, 1))
            placed = named("placed", (2,))
            turned_up = named("turned_up", (2,))
            block_taken = named("block_taken", (2,))
            cleared = named("cleared", (0, 1))
            return (in_ready, rows_ready, hidden_out, added, preset, hid_mm, hid_ready, w_done, mult_done,
                    same_ready, msg_ready, summed, sums_taken, dest_ready, shifted, offset_ready, turned, filled,
                    reduced, att_ready, measured, reads_ready, rows_mm, rows_taken, placed, turned_up, block_taken, cleared)

        def edge_pass(layer, windowed, semaphores):
            (in_ready, rows_ready, hidden_out, added, preset, hid_mm, hid_ready, w_done, mult_done,
             same_ready, msg_ready, summed, sums_taken, dest_ready, shifted, offset_ready, turned, filled,
             reduced, att_ready, measured, reads_ready, rows_mm, rows_taken, placed, turned_up, block_taken, cleared) = semaphores
            conv = layer < 2
            gw = (NS, F0, NS)[layer]
            table = (x_tab, sv_tab, x1_tab)[layer]
            ni, nj = ((NS, J), (J, NS), (NS, NS + 1))[layer]
            wcols = ni * nj
            fw = (F0, F1, F0)[layer]
            acc = (acc0, acc1, acc2)[layer]
            start = (4, 0, 1)[layer]
            mw = start + fw
            key, to, frm = (0, 1, 0) if conv else (1, 0, 1)
            by_window, into_window = windowed and conv, windowed and not conv
            find_dests = not into_window and layer != 1
            with ExitStack() as st:
                name = lambda s: f"{s}_{layer}{'w' if windowed else ''}"
                idx = sb(name("idx"), [P, U, 2, G], I32, on=st)
                rows = sb(name("rows"), [P, U, G, gw], on=st)
                prod = sb(name("prod"), [P, U, G, wcols], on=st)
                msg = sb(name("msg"), [P, U, G, mw], on=st)
                ps_w = ps(name("ps_w"), [P, G, BANK], on=st)
                ps_sum = ps(name("ps_sum"), [P, 3 if into_window else 1, BANK], on=st)
                if layer == 0 or by_window:
                    ps_in = ps(name("ps_in"), [P, 2 if layer == 0 else 1, BANK], on=st)
                if into_window:
                    in_window = sb(name("in_window"), [P, U, G, P], on=st)
                    table_sb = sb(name("table_sb"), [F0, NPAD + P], on=st)
                else:
                    keys = sb(name("keys"), [P, U, GE], U16, on=st)
                    same = sb(name("same"), [P, U, G, P], on=st)
                    later = sb(name("later"), [P, U, G], on=st)
                    from_spare = sb(name("from_spare"), [P, U, G], on=st)
                    dest = sb(name("dest"), [P, U, G], I32, on=st)
                    sums = sb(name("sums"), [P, U, G, fw], on=st)
                if windowed:
                    distance = sb(name("distance"), [P, GE], on=st)
                if by_window:
                    targets = sb(name("targets"), [P, U, GE], U16, on=st)
                    reads = sb(name("reads"), [P, U, GE], BF16, on=st)
                    window = sb(name("window"), [P, U, 3, gw], BF16, on=st)
                if conv:
                    hid = sb(name("hid"), [P, U, GE], on=st)
                    turn_prod = sb(name("turn_prod"), [P, U, G, 3 * NV], on=st)
                else:
                    types = sb(name("types"), [P, U, GE], U16, on=st)
                    onehot = sb(name("onehot"), [P, U, GE], BF16, on=st)
                    he_sb = sb(name("he_sb"), [P, U, G, NS], on=st)
                    he_prod = sb(name("he_prod"), [P, U, G, NS], on=st)
                    edge = sb(name("edge"), [P, U, G], on=st)
                    att = sb(name("att"), [P, U, G], on=st)
                if layer == 0:
                    feat = sb(name("feat"), [P, U, GE], on=st)
                block = st.enter_context(nc.Block())
                dests = 2 if layer == 0 else 1
                presets = 2 if conv else 0
                clears = acc1 if layer == 0 else acc2 if layer == 1 and not windowed else []
                clearing = [0]
                loads = 3 + (layer == 2) + 2 * by_window - into_window

                @block.sync
                def _(sp):
                    def load(turn, u):
                        n = turn * U + u
                        if layer == 0:
                            need(sp, hid_mm, n - U + 1)
                        if layer == 1:
                            need(sp, w_done, 2 * (n - U + 1))
                            sp.sem_inc(passed)
                        if not conv:
                            need(sp, hid_ready, n - U + 1)
                            need(sp, turned, n - U + 1)
                        if by_window:
                            need(sp, rows_mm, n - U + 1)
                        if find_dests:
                            need(sp, offset_ready, n - U + 1)
                        elif not into_window:
                            need(sp, same_ready, n - U + 1)
                        sp.sem_inc(passed)
                        if not by_window:
                            need(sp, rows_ready[u], 16 * G * turn)
                            sp.sem_inc(passed)
                        e0 = n * GE
                        sp.dma_start(idx[:, u], meta[bass.ds(n, 1)].rearrange("a p k g -> (a p) k g")).then_inc(in_ready[u], 16)
                        if layer == 0:
                            sp.dma_start(feat[0:DE, u, :], eaT[:, bass.ds(e0, GE)]).then_inc(in_ready[u], 16)
                        elif layer == 1:
                            sp.dma_start(hid[0:DE, u, :], hidden1[:, bass.ds(e0, GE)]).then_inc(in_ready[u], 16)
                        else:
                            sp.dma_start(he_sb[:, u], he[bass.ds(n, 1)].rearrange("a p g f -> (a p) g f")).then_inc(in_ready[u], 16)
                            sp.dma_start(types[:, u, :], short[2:3, bass.ds(e0, GE)].partition_broadcast(P)).then_inc(in_ready[u], 16)
                        if by_window:
                            sp.dma_start(targets[:, u, :], short[1:2, bass.ds(e0, GE)].partition_broadcast(P)).then_inc(in_ready[u], 16)
                            base = sp.value_load(first[0:1, bass.ds(n, 1)], min_val=0, max_val=N - 1)
                            sp.dma_start(window[:, u].rearrange("p k f -> p (k f)"),
                                         (x_parts, sv_parts)[layer][bass.ds(base, P), :]).then_inc(in_ready[u], 16)
                        if not into_window:
                            sp.dma_start(keys[:, u, :], short[key:key + 1, bass.ds(e0, GE)].partition_broadcast(P)).then_inc(in_ready[u], 16)

                    def store_hidden(turn, u):
                        n = turn * U + u
                        need(sp, hid_ready, n + 1)
                        sp.sem_inc(passed)
                        sp.dma_start(hidden1[:, bass.ds(n * GE, GE)], hid[DE:DH, u, :]).then_inc(hidden_out[u], 16)
                    for a in clears:
                        for half in range(a.shape[1] // F1):
                            width = ROWS * F1 // P
                            sp.dma_start(a.rearrange("(p r) f -> p (r f)", p=P)[:, half * width:(half + 1) * width],
                                         x1_all[:].rearrange("p b f -> p (b f)")).then_inc(cleared, 16)
                            clearing[0] += 16
                    need(sp, preset, presets)
                    pipelined(sp, [(0, load)] + ([(2, store_hidden)] if layer == 0 else []))
                    if layer == 0:
                        for u in range(U):
                            sp.wait_ge(hidden_out[u], 16 * TURNS)
                    if clears:
                        sp.wait_ge(cleared, clearing[0])

                @block.gpsimd
                def _(pool):
                    if layer == 0:
                        nc.gpsimd.memset(feat[:], 0.0).then_inc(preset, 1)
                    if layer == 1:
                        nc.gpsimd.memset(hid[DH:P, :, :], 1.0).then_inc(preset, 1)

                    def gather(turn, u):
                        n = turn * U + u
                        need(pool, in_ready[u], 16 * loads * (turn + 1))
                        need(pool, mult_done, 2 * (n - U + 1))
                        pool.sem_inc(passed)
                        for g in range(G):
                            nc.gpsimd.indirect_dma_start(
                                out=rows[:, u, g, :], out_offset=None, in_=table,
                                in_offset=bass.IndirectOffsetOnAxis(ap=idx[:, u, frm, g:g + 1], axis=0),
                            ).then_inc(rows_ready[u], 16)

                    def add(turn, u):
                        n = turn * U + u
                        need(pool, sums_taken, n + 1)
                        need(pool, dest_ready, (n + 1) * dests)
                        for g in range(G):
                            need(pool, added[g], 16 * n)
                            pool.sem_inc(passed)
                            nc.gpsimd.indirect_dma_start(
                                out=acc[g], out_offset=bass.IndirectOffsetOnAxis(ap=dest[:, u, g:g + 1], axis=0),
                                in_=sums[:, u, g, :], in_offset=None, compute_op=ALU.add,
                            ).then_inc(added[g], 16)
                    pipelined(pool, ([] if by_window else [(0, gather)]) + ([] if into_window else [(5, add)]))
                    if not into_window:
                        for g in range(G):
                            pool.wait_ge(added[g], 16 * NG)

                @block.tensor
                def _(pe):
                    def hidden(turn, u):
                        n = turn * U + u
                        need(pe, in_ready[u], 16 * loads * (turn + 1))
                        need(pe, hid_ready, n)
                        if by_window:
                            need(pe, rows_taken, n)
                        pe.sem_inc(passed)
                        for c in range(2):
                            mm = nc.tensor.matmul(ps_in[0:DH, c, 0:GE // 2], w1_sb[:],
                                                  feat[:, u, c * (GE // 2):(c + 1) * (GE // 2)], start=True, stop=True)
                        mm.then_inc(hid_mm, 1)

                    def read_window(turn, u):
                        n = turn * U + u
                        need(pe, in_ready[u], 16 * loads * (turn + 1))
                        need(pe, reads_ready, n + 1)
                        need(pe, rows_taken, n)
                        for g in range(G):
                            for k in range(3):
                                mm = nc.tensor.matmul(ps_in[:, 0, ROWS_AT + g * gw:ROWS_AT + (g + 1) * gw],
                                                      reads[:, u, g * P:(g + 1) * P], window[:, u, k, :], start=k == 0, stop=k == 2)
                        mm.then_inc(rows_mm, 1)

                    def weights(turn, u, g):
                        n = turn * U + u
                        if g == 0:
                            if layer == 1:
                                need(pe, in_ready[u], 16 * loads * (turn + 1))
                            else:
                                need(pe, hid_ready, n + 1)
                        for b, (g0, g1) in enumerate(BATCHES):
                            if g == g0:
                                need(pe, mult_done, 2 * n - 1 + b)
                        if conv:
                            mm = nc.tensor.matmul(ps_w[:, g, 0:wcols], hid[:, u, g * P:(g + 1) * P], w2_sb[:, layer, :],
                                                  start=True, stop=True)
                        else:
                            for k in range(3):
                                mm = nc.tensor.matmul(ps_w[:, g, 0:wcols], onehot[:, u, g * P:(g + 1) * P],
                                                      rel_parts[:, k, :], start=k == 0, stop=k == 2)
                        if any(g == g1 - 1 for _, g1 in BATCHES):
                            mm.then_inc(w_done, 1)

                    def sum_messages(turn, u, g):
                        n = turn * U + u
                        if g == 0:
                            need(pe, msg_ready, n + 1)
                            need(pe, same_ready, n + 1)
                            if into_window:
                                need(pe, placed, n - 1)
                            else:
                                need(pe, sums_taken, n)
                        if into_window:
                            mm = nc.tensor.matmul(ps_sum[0:fw, u % 3, 0:P], msg[:, u, g, start:start + fw], in_window[:, u, g, :],
                                                  start=g == 0, stop=g == G - 1)
                        else:
                            mm = nc.tensor.matmul(ps_sum[:, 0, g * fw:(g + 1) * fw], same[:, u, g, :],
                                                  msg[:, u, g, start:start + fw], start=True, stop=True)
                        if g == G - 1:
                            mm.then_inc(summed, 1)

                    def turn_and_sum(turn, u):
                        before, slot = turn + (u - LATE) // U, (u - LATE) % U
                        for g in range(G):
                            if not (isinstance(turn, int) and turn >= TURNS):
                                weights(turn, u, g)
                            if not (isinstance(before, int) and before < 0):
                                sum_messages(before, slot, g)

                    need(pe, preset, presets)
                    pipelined(pe, ([(0, hidden)] if layer == 0 else []) + ([(0, read_window)] if by_window else [])
                              + [(1, turn_and_sum)])
                    for u in range(LATE):
                        turn_and_sum(TURNS, u)
                    if into_window:
                        by_block = table_sb[:, 0:NPAD].rearrange("f (p b) -> f b p", b=BLK)
                        for k in range(BLK // BATCH):
                            need(pe, placed, NG)
                            need(pe, block_taken, k - G + 1)
                            for m in range(BATCH):
                                b = k * BATCH + m
                                mm = nc.tensor.transpose(ps_w[:, k % G, m * F0:(m + 1) * F0], by_block[:, b, :], eye[:])
                            mm.then_inc(turned_up, 1)

                @block.scalar
                def _(act):
                    def find_reads(turn, u):
                        n = turn * U + u
                        need(act, in_ready[u], 16 * loads * (turn + 1))
                        need(act, reads_ready, n)
                        nc.scalar.activation(distance[:], targets[:, u, :], ACT.Abs,
                                             bias=minus_node[:, bass.ds(n, 1)]).then_inc(measured, 1)
                        need(act, measured, n + 1)
                        need(act, rows_mm, n - U + 1)
                        nc.scalar.activation(reads[:, u, :], distance[:], ACT.Relu, bias=ones[:, 0:1],
                                             scale=-1.0).then_inc(reads_ready, 1)

                    def find_place(turn, u):
                        n = turn * U + u
                        need(act, same_ready, n)
                        for g in range(G):
                            ins = nc.scalar.activation(distance[:, g * P:(g + 1) * P], places[:], ACT.Abs,
                                                       bias=from_first[:, bass.ds(n * G + g, 1)], scale=-1.0)
                        ins.then_inc(measured, 1)
                        need(act, measured, n + 1)
                        need(act, summed, n - U + 1)
                        nc.scalar.activation(in_window[:, u].rearrange("p g r -> p (g r)"), distance[:], ACT.Relu,
                                             bias=ones[:, 0:1], scale=-1.0).then_inc(same_ready, 1)

                    def relu(turn, u):
                        n = turn * U + u
                        need(act, hid_mm, n + 1)
                        if by_window:
                            need(act, rows_mm, n + 1)
                        need(act, w_done, 2 * (n - U + 1))
                        need(act, hidden_out[u], 16 * turn)
                        nc.scalar.activation(hid[0:DH, u, :].rearrange("p (c e) -> p c e", c=2), ps_in[0:DH, :, 0:GE // 2],
                                             ACT.Relu, bias=b1_sb[:]).then_inc(hid_ready, 1)

                    def shift(turn, u):
                        n = turn * U + u
                        need(act, in_ready[u], 16 * loads * (turn + 1))
                        need(act, offset_ready, n - U + 1)
                        nc.scalar.activation(from_spare[:, u, :], idx[:, u, to, :], ACT.Identity, bias=minus_spare[:]).then_inc(shifted, 1)

                    def take_rows(turn, u):
                        n = turn * U + u
                        need(act, rows_mm, n + 1)
                        need(act, mult_done, 2 * (n - U + 1))
                        nc.scalar.activation(rows[:, u].rearrange("p g f -> p (g f)"), ps_in[:, 0, ROWS_AT:ROWS_AT + G * gw],
                                             ACT.Copy).then_inc(rows_taken, 1)

                    def take_sums(turn, u):
                        n = turn * U + u
                        need(act, summed, n + 1)
                        for g in range(G):
                            need(act, added[g], 16 * (n - U + 1))
                        nc.scalar.activation(sums[:, u].rearrange("p g f -> p (g f)"), ps_sum[:, 0, 0:G * fw],
                                             ACT.Copy).then_inc(sums_taken, 1)
                        if find_dests:
                            need(act, offset_ready, n + 1)
                            nc.scalar.activation(dest[:, u, :], later[:, u, :], ACT.Identity, bias=spare[:]).then_inc(dest_ready, 1)
                        if layer == 0:
                            nc.scalar.activation(dest_all[:, bass.ds(n * G, G)], later[:, u, :], ACT.Identity,
                                                 bias=spare[:]).then_inc(dest_ready, 1)
                        if layer == 1:
                            nc.scalar.activation(dest[:, u, :], dest_all[:, bass.ds(n * G, G)], ACT.Copy).then_inc(dest_ready, 1)
                    need(act, preset, presets)
                    if into_window:
                        pipelined(act, [(0, find_place)])
                    else:
                        pipelined(act, ([(0, find_reads)] if by_window else []) + ([(0, shift)] if find_dests else [])
                                  + [(5, take_sums)]
                                  + ([(0, relu)] if layer == 0 else []) + ([(0, take_rows)] if by_window else []))

                @block.vector
                def _(dve):
                    if layer == 1:
                        nc.vector.memset(hid[0:DH, :, :], 0.0)
                    if layer == 0:
                        nc.vector.memset(hid[DH:P, :, :], 1.0)
                        nc.vector.memset(msg[:, :, :, J + 3 * NV:J + 3 * NV + 1], 1.0)
                        nc.vector.memset(msg[:, :, :, J + 3 * NV + 1:], 0.0)
                    if into_window:
                        nc.vector.memset(table_sb[:], 0.0)
                    nc.vector.drain().then_inc(preset, 1)
                    need(dve, preset, presets if conv else 1)

                    def find_same(turn, u):
                        n = turn * U + u
                        need(dve, in_ready[u], 16 * loads * (turn + 1))
                        need(dve, summed, n - U + 1)
                        if find_dests:
                            need(dve, dest_ready, (n - U + 1) * dests)
                            for g in range(G):
                                ins = nc.vector.scalar_tensor_tensor(
                                    out=same[:, u, g, :], in0=keys[:, u, g * P:(g + 1) * P], scalar=idx[:, u, to, g:g + 1],
                                    in1=upper[:], op0=ALU.is_equal, op1=ALU.mult, accum_out=later[:, u, g:g + 1])
                        else:
                            ins = nc.vector.tensor_tensor(same[:, u], keys[:, u, :].rearrange("p (g e) -> p g e", g=G),
                                                          idx[:, u, to, :].unsqueeze(2).broadcast_to([P, G, P]), ALU.is_equal)
                        ins.then_inc(same_ready, 1)

                    def find_offset(turn, u):
                        n = turn * U + u
                        need(dve, same_ready, n + 1)
                        need(dve, shifted, n + 1)
                        nc.vector.scalar_tensor_tensor(out=later[:, u, :], in0=later[:, u, :], scalar=1.0, in1=from_spare[:, u, :],
                                                       op0=ALU.is_equal, op1=ALU.mult).then_inc(offset_ready, 1)

                    def place(turn, u):
                        n = turn * U + u
                        base = dve.value_load(first[0:1, bass.ds(n, 1)], min_val=0, max_val=N - 1)
                        part = table_sb[:, bass.ds(base, P)]
                        need(dve, placed, n)
                        need(dve, summed, n + 1)
                        nc.vector.tensor_tensor(part, ps_sum[0:fw, u % 3, 0:P], part, ALU.add).then_inc(placed, 1)

                    def find_type(turn, u):
                        n = turn * U + u
                        need(dve, in_ready[u], 16 * loads * (turn + 1))
                        need(dve, w_done, 2 * (n - U + 1))
                        nc.vector.tensor_scalar(onehot[:, u, :], types[:, u, :], lane[:], None,
                                                ALU.is_equal).then_inc(hid_ready, 1)

                    def edge_products(turn, u):
                        nc.vector.tensor_tensor(he_prod[:, u], he_sb[:, u],
                                                u_all[:, 1:2, :].broadcast_to([P, G, NS]), ALU.mult).then_inc(turned, 1)

                    def edge_sums(turn, u):
                        need(dve, turned, turn * U + u + 1)
                        nc.vector.reduce_sum(edge[:, u, :], he_prod[:, u], AX.X).then_inc(filled, 1)

                    def rows_here(turn, u):
                        n = turn * U + u
                        if by_window:
                            need(dve, rows_taken, n + 1)
                        else:
                            need(dve, rows_ready[u], 16 * G * (turn + 1))

                    def directions(n):
                        return rhat[:, bass.ds(n * G, G), :].unsqueeze(2).broadcast_to([P, G, NV, 3])

                    def along_products(turn, u):
                        n = turn * U + u
                        rows_here(turn, u)
                        nc.vector.tensor_tensor(turn_prod[:, u].rearrange("p g (k c) -> p g k c", c=3),
                                                rows[:, u, :, J:F0].rearrange("p g (k c) -> p g k c", c=3),
                                                directions(n), ALU.mult).then_inc(turned, 1)

                    def along_sums(turn, u):
                        need(dve, turned, turn * U + u + 1)
                        nc.vector.reduce_sum(rows[:, u, :, NS:J], turn_prod[:, u].rearrange("p g (k c) -> p g k c", c=3),
                                             AX.X).then_inc(filled, 1)

                    def multiply(turn, u, b):
                        n = turn * U + u
                        g0, g1 = BATCHES[b]
                        if b == 0:
                            rows_here(turn, u)
                            if layer == 1:
                                need(dve, filled, n + 1)
                        need(dve, w_done, 2 * n + 1 + b)
                        nc.vector.tensor_tensor(
                            prod[:, u, g0:g1, :].rearrange("p g (j i) -> p g j i", i=ni),
                            ps_w[:, g0:g1, 0:wcols].rearrange("p g (j i) -> p g j i", i=ni),
                            rows[:, u, g0:g1, 0:ni].unsqueeze(2).broadcast_to([P, g1 - g0, nj, ni]),
                            ALU.mult).then_inc(mult_done, 1)

                    def multiply_first(turn, u):
                        multiply(turn, u, 0)

                    def multiply_second(turn, u):
                        multiply(turn, u, 1)

                    def reduce(turn, u):
                        n = turn * U + u
                        need(dve, mult_done, 2 * (n + 1))
                        need(dve, summed, n - U + 1)
                        nc.vector.reduce_sum(msg[:, u, :, 0:nj], prod[:, u].rearrange("p g (j i) -> p g j i", i=ni),
                                             AX.X).then_inc(msg_ready if layer == 1 else reduced, 1)

                    def vectors(turn, u):
                        n = turn * U + u
                        need(dve, reduced, n + 1)
                        nc.vector.tensor_tensor(msg[:, u, :, J:J + 3 * NV].rearrange("p g (k c) -> p g k c", c=3),
                                                msg[:, u, :, 0:NV].unsqueeze(3).broadcast_to([P, G, NV, 3]),
                                                directions(n), ALU.mult).then_inc(msg_ready, 1)

                    def attention(turn, u):
                        n = turn * U + u
                        need(dve, reduced, n + 1)
                        need(dve, filled, n + 1)
                        nc.vector.tensor_tensor(att[:, u, :], msg[:, u, :, 0], edge[:, u, :], ALU.add).then_inc(att_ready, 1)

                    def attend(turn, u):
                        n = turn * U + u
                        need(dve, att_ready, n + 1)
                        nc.vector.tensor_tensor(msg[:, u, :, nj:], msg[:, u, :, 1:nj],
                                                att[:, u, :].unsqueeze(2).broadcast_to([P, G, NS]),
                                                ALU.mult).then_inc(msg_ready, 1)

                    if layer == 0:
                        pipelined(dve, [(0, find_same), (2, vectors), (0, multiply_first), (0, multiply_second),
                                        (0, find_offset), (1, reduce)])
                    elif layer == 1:
                        pipelined(dve, [(0, along_products), (0, find_same), (0, along_sums), (1, reduce),
                                        (0, multiply_first), (0, multiply_second)])
                    else:
                        pipelined(dve, [(0, find_type), (1, edge_products)] + ([] if into_window else [(1, find_same)])
                                  + [(1, edge_sums)] + ([(5, place)] if into_window else []) + [(3, attend), (1, multiply_first)]
                                  + [(1, multiply_second)] + ([] if into_window else [(1, find_offset)]) + [(2, reduce), (2, attention)])
                    if into_window:
                        for k in range(BLK // BATCH):
                            need(dve, turned_up, k + 1)
                            nc.vector.tensor_copy(table_rows[:, k * BATCH:(k + 1) * BATCH, :].rearrange("p b f -> p (b f)"),
                                                  ps_w[:, k % G, 0:BATCH * F0]).then_inc(block_taken, 1)

        def node_semaphores(layer, st):
            tables = G if layer < 2 else 1
            return ([[sem(f"table_in{g}_n{layer}", st) for g in range(tables)]]
                    + [sem(f"{what}_n{layer}", st) if layer < 2 else None for what in ("partial", "total")]
                    + [sem(f"{what}_n{layer}", st) for what in ("square", "rooted", "step", "stored", "finished")])

        def node_stage(layer, semaphores, summed_up=False):
            table_in, partial, total, square, rooted, step, stored, finished = semaphores
            fw = (F0, F1, F0)[layer]
            acc = (acc0, acc1, acc2)[layer]
            with ExitStack() as st:
                name = lambda s: f"{s}_n{layer}{'w' if summed_up else ''}"
                if summed_up:
                    tot = table_rows
                else:
                    parts = sb(name("parts"), [P, G, BLK, fw], on=st)
                    tot = sb(name("tot"), [P, BLK, fw], on=st)[:]
                y = sb(name("y"), [P, BLK, F0], on=st)
                sq = sb(name("sq"), [P, BLK, F0], on=st)
                row = sb(name("row"), [P, 4, F0], on=st)
                per = sb(name("per"), [P, 6, BLK], on=st)
                ps_t = ps(name("ps_t"), [P, 2, BANK], on=st)
                n_tot = (2, 2, 0)[layer]
                roots = (1, 2, 1)[layer]
                block = st.enter_context(nc.Block())
                ncol = J if layer == 0 else NS
                if layer == 0:
                    sv_split = (parts[:, 2:4].rearrange("p g b f -> p (g b f)")[:, 0:BLK * 3 * F0 // 2].bitcast(BF16)
                                .rearrange("p (b k f) -> p b k f", k=3, f=F0))
                of_columns = (row[:, 1, 0:ncol], row[:, 2, 0:ncol])
                of_nodes = (per[:, 1, :], per[:, 2, :])
                rounds = ([of_columns], [of_columns, of_nodes], [of_nodes])[layer]

                @block.sync
                def _(sp):
                    for g in range(0 if summed_up else G):
                        sp.dma_start(parts[:, g], acc[g][0:NPAD, :].rearrange("(p b) f -> p b f", p=P)).then_inc(table_in[g % len(table_in)], 16)
                    sp.wait_ge(finished, 1)
                    if layer == 0:
                        sp.dma_start(sv_tab[0:NPAD, :].rearrange("(p b) f -> p b f", p=P), y[:]).then_inc(stored, 16)
                        sp.dma_start(sv_parts[0:NPAD, :].rearrange("(p b) f -> p b f", p=P),
                                     sv_split.rearrange("p b k f -> p b (k f)")).then_inc(stored, 16)
                        sp.wait_ge(stored, 32)
                    elif layer == 1:
                        sp.dma_start(x1_tab.rearrange("(p b) f -> p b f", p=P), x1_sb).then_inc(stored, 16)
                        sp.wait_ge(stored, 16)
                    else:
                        sp.dma_start(out[0:(P - 1) * BLK, :].rearrange("(p b) f -> p b f", p=P - 1),
                                     x_sb[0:P - 1]).then_inc(stored, 16)
                        sp.dma_start(out[(P - 1) * BLK:N, :].rearrange("(p b) f -> p b f", p=1),
                                     x_sb[P - 1:P, 0:LAST, :]).then_inc(stored, 16)
                        sp.wait_ge(stored, 32)

                @block.tensor
                def _(pe):
                    for k in range(n_tot):
                        pe.wait_ge(partial, k + 1)
                        nc.tensor.matmul(ps_t[:, k, 0:F0], ones[:], row[:, 0, :], start=True, stop=True).then_inc(total, 1)

                @block.scalar
                def _(act):
                    for k, (square_of, root_of) in enumerate(rounds):
                        act.wait_ge(square, k + 1)
                        nc.scalar.activation(root_of, square_of, ACT.Sqrt).then_inc(rooted, 1)

                @block.vector
                def _(dve):
                    done = [0]

                    def chain(ins):
                        ins.then_inc(step, 1)
                        done[0] += 1
                        dve.wait_ge(step, done[0])

                    def over_nodes(k):
                        nc.vector.drain().then_inc(partial, 1)
                        dve.wait_ge(total, k + 1)

                    def inverse_root(a, root, out_, spare_, k):
                        nc.vector.drain().then_inc(square, 1)
                        dve.wait_ge(rooted, k + 1)
                        chain(nc.vector.reciprocal(spare_, root))
                        chain(nc.vector.tensor_tensor(spare_, spare_, a, ALU.mult))
                        chain(nc.vector.tensor_tensor(spare_, spare_, root, ALU.add))
                        chain(nc.vector.tensor_scalar(spare_, spare_, 0.5, None, ALU.mult))
                        chain(nc.vector.reciprocal(out_, spare_))

                    def rows_of(a):
                        return a.unsqueeze(1).broadcast_to([P, BLK, a.shape[-1]])

                    def layernorm(dst, src):
                        chain(nc.vector.reduce_sum(per[:, 0, :], src, AX.X))
                        chain(nc.vector.tensor_scalar(per[:, 0, :], per[:, 0, :], 1.0 / NS, None, ALU.mult))
                        chain(nc.vector.tensor_tensor(src, src, per[:, 0, :].unsqueeze(2).broadcast_to([P, BLK, NS]), ALU.subtract))
                        chain(nc.vector.tensor_tensor(sq[:, :, 0:NS], src, src, ALU.mult))
                        chain(nc.vector.reduce_sum(per[:, 1, :], sq[:, :, 0:NS], AX.X))
                        chain(nc.vector.tensor_scalar(per[:, 1, :], per[:, 1, :], 1.0 / NS, EPS, ALU.mult, ALU.add))
                        inverse_root(per[:, 1, :], per[:, 2, :], per[:, 3, :], per[:, 4, :], roots - 1)
                        chain(nc.vector.tensor_tensor(dst, src, per[:, 3, :].unsqueeze(2).broadcast_to([P, BLK, NS]), ALU.mult))

                    if not summed_up:
                        loaded = 16 * G // len(table_in)
                        dve.wait_ge(table_in[0], loaded)
                        for g in range(1, G):
                            if len(table_in) > 1:
                                dve.wait_ge(table_in[g], loaded)
                            chain(nc.vector.tensor_tensor(tot, tot if g > 1 else parts[:, 0], parts[:, g], ALU.add))
                    if layer < 2:
                        if layer == 0:
                            chain(nc.vector.tensor_scalar(inv_count[:], tot[:, :, NS + 3 * NV], 1.0, None, ALU.max))
                            chain(nc.vector.reciprocal(inv_count[:], inv_count[:]))
                        scale = 0.25 if layer == 0 else float((NS + NV) ** -0.5)
                        chain(nc.vector.tensor_scalar(per[:, 5, :], inv_count[:], scale, None, ALU.mult))
                        chain(nc.vector.tensor_tensor(y[:, :, 0:NS], tot[:, :, 0:NS],
                                                      per[:, 5, :].unsqueeze(2).broadcast_to([P, BLK, NS]), ALU.mult))
                        chain(nc.vector.memset(row[:], 0.0))
                        chain(nc.vector.reduce_sum(row[:, 0, 0:NS], y[:, :, 0:NS].rearrange("p b f -> p f b"), AX.X))
                        over_nodes(0)
                        chain(nc.vector.tensor_scalar(row[:, 3, 0:NS], ps_t[:, 0, 0:NS], 1.0 / N, None, ALU.mult))
                        chain(nc.vector.tensor_tensor(y[:, :, 0:NS], y[:, :, 0:NS], rows_of(row[:, 3, 0:NS]), ALU.subtract))
                        chain(nc.vector.tensor_tensor(y[:, :, 0:NS], y[:, :, 0:NS],
                                                      mask[:, :].unsqueeze(2).broadcast_to([P, BLK, NS]), ALU.mult))
                        chain(nc.vector.tensor_tensor(sq[:, :, 0:NS], y[:, :, 0:NS], y[:, :, 0:NS], ALU.mult))
                        chain(nc.vector.reduce_sum(row[:, 0, 0:NS], sq[:, :, 0:NS].rearrange("p b f -> p f b"), AX.X))
                        if layer == 0:
                            chain(nc.vector.tensor_scalar(per[:, 5, :], inv_count[:], 0.25 * 3.0 ** 0.5, None, ALU.mult))
                            chain(nc.vector.tensor_tensor(y[:, :, J:F0], tot[:, :, NS:NS + 3 * NV],
                                                          per[:, 5, :].unsqueeze(2).broadcast_to([P, BLK, 3 * NV]), ALU.mult))
                            chain(nc.vector.tensor_tensor(sq[:, :, J:F0], y[:, :, J:F0], y[:, :, J:F0], ALU.mult))
                            chain(nc.vector.reduce_sum(row[:, 1, 0:3 * NV], sq[:, :, J:F0].rearrange("p b f -> p f b"), AX.X))
                            chain(nc.vector.reduce_sum(row[:, 0, NS:J], row[:, 1, 0:3 * NV].rearrange("p (k c) -> p k c", c=3), AX.X))
                        over_nodes(1)
                        chain(nc.vector.tensor_scalar(row[:, 1, 0:NS], ps_t[:, 1, 0:NS], 1.0 / N, EPS, ALU.mult, ALU.add))
                        if layer == 0:
                            chain(nc.vector.tensor_scalar(row[:, 1, NS:J], ps_t[:, 1, NS:J], 1.0 / (3 * N), EPS, ALU.mult, ALU.add))
                        inverse_root(row[:, 1, 0:ncol], row[:, 2, 0:ncol], row[:, 3, 0:ncol], row[:, 0, 0:ncol], 0)
                        gains = bn0_sb if layer == 0 else bn1_sb
                        chain(nc.vector.tensor_tensor(row[:, 0, 0:NS], row[:, 3, 0:NS], gains[:, 0:NS], ALU.mult))
                        chain(nc.vector.tensor_tensor(y[:, :, 0:NS], y[:, :, 0:NS], rows_of(row[:, 0, 0:NS]), ALU.mult))
                        chain(nc.vector.tensor_tensor(y[:, :, 0:NS], y[:, :, 0:NS], rows_of(gains[:, NS:2 * NS]), ALU.add))
                        if layer == 0:
                            chain(nc.vector.tensor_tensor(row[:, 0, NS:J], row[:, 3, NS:J], gains[:, 2 * NS:], ALU.mult))
                            chain(nc.vector.tensor_tensor(
                                y[:, :, J:F0].rearrange("p b (k c) -> p b k c", c=3), y[:, :, J:F0].rearrange("p b (k c) -> p b k c", c=3),
                                row[:, 0, NS:J].unsqueeze(1).unsqueeze(3).broadcast_to([P, BLK, NV, 3]), ALU.mult))
                            chain(nc.vector.memset(y[:, :, NS:J], 0.0))
                            split_rows(chain, y[:], sv_split, [parts[:, 0], parts[:, 1]])
                        else:
                            chain(nc.vector.tensor_tensor(y[:, :, 0:NS], y[:, :, 0:NS], x_sb[:], ALU.add))
                            layernorm(x1_sb, y[:, :, 0:NS])
                    else:
                        chain(nc.vector.tensor_tensor(sq[:, :, 0:NS], x1_sb, rows_of(u_all[:, 2, :]), ALU.mult))
                        chain(nc.vector.reduce_sum(per[:, 5, :], sq[:, :, 0:NS], AX.X))
                        chain(nc.vector.tensor_tensor(y[:, :, 0:NS], tot[:, :, 0:NS],
                                                      per[:, 5, :].unsqueeze(2).broadcast_to([P, BLK, NS]), ALU.mult))
                        chain(nc.vector.tensor_tensor(y[:, :, 0:NS], y[:, :, 0:NS], tot[:, :, NS:], ALU.add))
                        chain(nc.vector.tensor_tensor(y[:, :, 0:NS], y[:, :, 0:NS], x1_sb, ALU.add))
                        layernorm(x_sb[:], y[:, :, 0:NS])
                    nc.vector.drain().then_inc(finished, 1)

        n_outside = nc.values_load(outside[0:1, 0:1], min_val=0, max_val=2 * E)
        for layer in range(3):
            with ExitStack() as st:
                semaphores = pass_semaphores(layer, st)
                node_sems = node_semaphores(layer, st)
                with nc.If(n_outside == 0):
                    edge_pass(layer, True, semaphores)
                    if layer == 2:
                        node_stage(layer, node_sems, summed_up=True)
                with nc.Else():
                    edge_pass(layer, False, semaphores)
                    if layer == 2:
                        node_stage(layer, node_sems)
                if layer < 2:
                    node_stage(layer, node_sems)


def kernel(x, src, dst, edge_attr_16, edge_attr_3, edge_attr_48, edge_type_90, L0_gnn_fc0_w1, L0_gnn_fc0_b1, L0_gnn_fc0_w2,
           L0_gnn_fc0_b2, L0_gnn_fc1_w1, L0_gnn_fc1_b1, L0_gnn_fc1_w2, L0_gnn_fc1_b2, L0_gnn_bn0_gs, L0_gnn_bn0_bs,
           L0_gnn_bn0_gv, L0_gnn_bn1_gs, L0_gnn_bn1_bs, L1_gnn_Ws, L1_gnn_Wa, L1_gnn_weight, L1_gnn_w_comp):
    import numpy as np
    import concourse.bacc as bacc
    from concourse.bass_utils import run_bass_kernel_spmd as run

    def tiles(a):
        return a.reshape(NT, P, *a.shape[1:]).swapaxes(0, 1)

    def groups(a):
        return a.reshape(NG, G, P).transpose(0, 2, 1)

    def second(w, b, by_output):
        w = np.concatenate([w, np.zeros((DH - DE, W), np.float32), b[None], np.zeros((P - DH - 1, W), np.float32)], 0)
        wa, wb = w[:, :NS * NS].reshape(-1, NS, NS), w[:, NS * NS:]
        if by_output:
            wb = wb.reshape(-1, NS, NV)
            return np.concatenate([wb, wa], 2).transpose(0, 2, 1).reshape(-1, W)
        wb = wb.reshape(-1, NV, NS)
        return np.concatenate([wa, wb], 1).transpose(0, 2, 1).reshape(-1, W)

    (x, src, dst, edge_attr_16, edge_attr_3, edge_attr_48, edge_type_90) = (
        np.asarray(a) for a in (x, src, dst, edge_attr_16, edge_attr_3, edge_attr_48, edge_type_90))
    f = np.asarray
    ins = {
        "x": x,
        "eaT": edge_attr_48.T,
        "he": edge_attr_16.reshape(NG, G, P, NS).transpose(0, 2, 1, 3),
        "ev": tiles(edge_attr_3),
        "indices": np.stack([src, dst, edge_type_90]),
        "dst_cols": tiles(dst),
        "dst_first": dst[None, ::GE],
        "meta": np.stack([groups(dst), groups(src)], 2),
        "w1": np.concatenate([np.concatenate([f(L0_gnn_fc0_w1), f(L0_gnn_fc1_w1)], 1), np.zeros((P - DE, DH), np.float32)], 0),
        "b1": np.concatenate([f(L0_gnn_fc0_b1), f(L0_gnn_fc1_b1)])[:, None],
        "w2": np.stack([second(f(L0_gnn_fc0_w2), f(L0_gnn_fc0_b2), True), second(f(L0_gnn_fc1_w2), f(L0_gnn_fc1_b2), False)], 1),
        "bn0": np.concatenate([f(L0_gnn_bn0_gs), f(L0_gnn_bn0_bs), f(L0_gnn_bn0_gv)])[None],
        "bn1": np.concatenate([f(L0_gnn_bn1_gs), f(L0_gnn_bn1_bs)])[None],
        "ws": f(L1_gnn_Ws),
        "wa": f(L1_gnn_Wa).reshape(3, NS).T,
        "basis": f(L1_gnn_weight).reshape(NS, NB, NS).transpose(1, 0, 2).reshape(NB, NS * NS),
        "comp": f(L1_gnn_w_comp).T,
    }
    ins = {k: np.ascontiguousarray(v) for k, v in ins.items()}
    nc = bacc.Bacc("TRN2", target_bir_lowering=False, num_devices=1)
    args = {k: nc.dram_tensor(k, v.shape, mybir.dt.from_np(v.dtype), kind="ExternalInput").ap() for k, v in ins.items()}
    out = nc.dram_tensor("out", (N, NS), FP32, kind="ExternalOutput").ap()
    build(nc, out=out, **args)
    return run(nc, [ins], core_ids=[0]).results[0]["out"]
```
